# Optimizing a Trainium2 kernel written in Bass

```python
import numpy as np
import jax
import jax.numpy as jnp

def _softmax(x, axis=-1):
    return jax.nn.softmax(x, axis=axis)

def _gelu(x):
    return jax.nn.gelu(x, approximate=True)

def _silu(x):
    return jax.nn.silu(x)

def _sigmoid(x):
    return jax.nn.sigmoid(x)

def _layernorm(x, axis=-1, eps=1e-05):
    m = jnp.mean(x, axis=axis, keepdims=True)
    v = jnp.var(x, axis=axis, keepdims=True)
    return (x - m) / jnp.sqrt(v + eps)

def _scatter_add(tgt, idx, src, axis=0):
    return tgt.at[idx].add(src)

def _segment_sum(src, seg, n):
    return jax.ops.segment_sum(src, seg, n)
kernel_name = 'mk_macaron_d2_jaxref_r8_b43e1a'

def setup_inputs(seed: int=0):
    np.random.seed(seed)
    _w = jnp.asarray

    def _L0_attn_setup():
        import jax, jax.numpy as jnp
        import numpy as np
        D = 128
        H = 16
        K = 64
        B = 4
        T = 128
        LAYER_ID = 12
        NUM_LAYERS = 24
        D_MIX = 32
        D_DECAY = 64

        def _bidir_shift(x):
            left = jnp.pad(x[:, :-1, :], ((0, 0), (1, 0), (0, 0)))
            right = jnp.pad(x[:, 1:, :], ((0, 0), (0, 1), (0, 0)))
            return 0.5 * (left + right)

        def _lion_attention(r, k, v, w):
            Tn = r.shape[2]
            cs = jnp.cumsum(w, axis=2)
            cs_b = cs - w
            shift_f = cs[:, :, Tn // 2:Tn // 2 + 1, :]
            shift_b = cs_b[:, :, Tn // 2:Tn // 2 + 1, :]
            cf = jnp.clip(cs - shift_f, -60.0, 60.0)
            cb = jnp.clip(cs_b - shift_b, -60.0, 60.0)
            A_f = jnp.einsum('bhik,bhjk->bhij', r * jnp.exp(cf), k * jnp.exp(-cf))
            A_b = jnp.einsum('bhik,bhjk->bhij', r * jnp.exp(-cb), k * jnp.exp(cb))
            idx = jnp.arange(Tn)
            lower = idx[:, None] >= idx[None, :]
            A = jnp.where(lower, A_f, A_b)
            return jnp.einsum('bhij,bhjk->bhik', A, v)
        key = jax.random.key(seed)
        ks = jax.random.split(key, 12)
        r01 = LAYER_ID / (NUM_LAYERS - 1)
        r10 = 1.0 - LAYER_ID / NUM_LAYERS
        ddd = jnp.arange(D, dtype=jnp.float32) / D
        maa = lambda p: (1.0 - ddd ** p).reshape(1, 1, D)
        inp = {}
        inp['x'] = jax.random.normal(ks[0], (B, T, D), jnp.float32)
        inp['time_maa_x'] = maa(r10)
        inp['time_maa_w'] = maa(r10)
        inp['time_maa_k'] = maa(r10)
        inp['time_maa_v'] = (1.0 - (ddd ** r10 + 0.3 * r01)).reshape(1, 1, D)
        inp['time_maa_r'] = maa(0.5 * r10)
        inp['time_maa_g'] = maa(0.5 * r10)
        inp['time_maa_w1'] = jax.random.uniform(ks[1], (D, D_MIX * 5), jnp.float32, -0.01, 0.01)
        inp['time_maa_w2'] = jax.random.uniform(ks[2], (5, D_MIX, D), jnp.float32, -0.01, 0.01)
        n = jnp.arange(D, dtype=jnp.float32)
        inp['time_decay'] = (-6.0 + 5.0 * (n / (D - 1)) ** (0.7 + 1.3 * r01)).reshape(1, 1, D)
        inp['time_decay_w1'] = jax.random.uniform(ks[3], (D, D_DECAY), jnp.float32, -0.01, 0.01)
        inp['time_decay_w2'] = jax.random.uniform(ks[4], (D_DECAY, D), jnp.float32, -0.01, 0.01)
        for nm, kk in zip(['W_r', 'W_k', 'W_v', 'W_g', 'W_o'], ks[5:10]):
            inp[nm] = jax.random.normal(kk, (D, D), jnp.float32) * 0.02
        inp['ln_w'] = jnp.ones((D,), jnp.float32)
        inp['ln_b'] = jnp.zeros((D,), jnp.float32)
        return inp
    _L0_attn_in = _L0_attn_setup()

    def _L0_ffn_setup():
        import jax, jax.numpy as jnp
        import numpy as np
        EPS = 1e-06
        LN_EPS = 1e-05

        def _absmean_core(W):
            gamma = jnp.mean(jnp.abs(W)) + EPS
            Ws = W / gamma
            Wq = jnp.sign(Ws) * jnp.minimum(jnp.round(jnp.abs(Ws)), 1.0)
            return (Wq, gamma)

        @jax.custom_vjp
        def absmean(W):
            return _absmean_core(W)[0]

        def _absmean_fwd(W):
            Wq, gamma = _absmean_core(W)
            return (Wq, gamma)

        def _absmean_bwd(gamma, g):
            return (g / gamma,)
        absmean.defvjp(_absmean_fwd, _absmean_bwd)

        def layernorm(x, w, b, eps=LN_EPS):
            mu = jnp.mean(x, axis=-1, keepdims=True)
            var = jnp.mean((x - mu) ** 2, axis=-1, keepdims=True)
            return (x - mu) * jax.lax.rsqrt(var + eps) * w + b
        key = jax.random.key(seed)
        k1, k2, k3 = jax.random.split(key, 3)
        d, h = (128, 512)
        B, T = (8, 256)
        return {'x': jax.random.normal(k1, (B, T, d), jnp.float32), 'W_fc': jax.random.normal(k2, (h, d), jnp.float32), 'ln_w': jnp.ones((h,), jnp.float32), 'ln_b': jnp.zeros((h,), jnp.float32), 'W_proj': jax.random.normal(k3, (d, h), jnp.float32)}
    _L0_ffn_in = _L0_ffn_setup()

    def _L1_attn_setup():
        import jax, jax.numpy as jnp
        import numpy as np
        from math import sqrt
        ROPE_BASE = 6000.0

        def _rope_tables(seq_len, rope_dim, dtype):
            inv_freq = 1.0 / ROPE_BASE ** (jnp.arange(0, rope_dim, 2, dtype=jnp.float32) / rope_dim)
            t = jnp.arange(seq_len, dtype=jnp.float32)
            freqs = jnp.outer(t, inv_freq)
            emb = jnp.concatenate([freqs, freqs], axis=-1)
            return (jnp.cos(emb).astype(dtype), jnp.sin(emb).astype(dtype))

        def _rotate_half(x):
            x1, x2 = jnp.split(x, 2, axis=-1)
            return jnp.concatenate([-x2, x1], axis=-1)
        key = jax.random.key(seed)
        k1, k2, k3 = jax.random.split(key, 3)
        B, S, D = (2, 256, 128)
        H, DK = (16, 64)
        x = jax.random.normal(k1, (B, S, D), dtype=jnp.float32)
        W_qkv = jax.random.normal(k2, (3, H, DK, D), dtype=jnp.float32) * 0.02
        W_o = jax.random.normal(k3, (D, H * DK), dtype=jnp.float32) * 0.02
        return {'x': x, 'W_qkv': W_qkv, 'W_o': W_o}
    _L1_attn_in = _L1_attn_setup()

    def _L1_ffn_setup():
        import jax, jax.numpy as jnp
        import numpy as np
        D_MODEL = 128
        D_FF = 512
        NUM_M = 2
        E_ROUTER = 8 * NUM_M - 1
        D_FF_R = D_FF // NUM_M
        TOP_K = NUM_M * 2 - 1
        B, T = (2, 256)

        def _expert_stack(x, W1, b1, W2, b2):
            h = jax.nn.gelu(jnp.einsum('btd,edf->ebtf', x, W1) + b1[:, None, None, :], approximate=False)
            return jnp.einsum('ebtf,efd->ebtd', h, W2) + b2[:, None, None, :]
        key = jax.random.key(seed)
        ks = jax.random.split(key, 12)
        s = lambda fan_in: 1.0 / np.sqrt(fan_in)
        x = jax.random.normal(ks[0], (B, T, D_MODEL), dtype=jnp.float32)
        sW1 = jax.random.uniform(ks[1], (1, D_MODEL, D_FF), jnp.float32, -s(D_MODEL), s(D_MODEL))
        sb1 = jax.random.uniform(ks[2], (1, D_FF), jnp.float32, -s(D_MODEL), s(D_MODEL))
        sW2 = jax.random.uniform(ks[3], (1, D_FF, D_MODEL), jnp.float32, -s(D_FF), s(D_FF))
        sb2 = jax.random.uniform(ks[4], (1, D_MODEL), jnp.float32, -s(D_FF), s(D_FF))
        rW1 = jax.random.uniform(ks[5], (E_ROUTER, D_MODEL, D_FF_R), jnp.float32, -s(D_MODEL), s(D_MODEL))
        rb1 = jax.random.uniform(ks[6], (E_ROUTER, D_FF_R), jnp.float32, -s(D_MODEL), s(D_MODEL))
        rW2 = jax.random.uniform(ks[7], (E_ROUTER, D_FF_R, D_MODEL), jnp.float32, -s(D_FF_R), s(D_FF_R))
        rb2 = jax.random.uniform(ks[8], (E_ROUTER, D_MODEL), jnp.float32, -s(D_FF_R), s(D_FF_R))
        gW = jax.random.uniform(ks[9], (D_MODEL, E_ROUTER), jnp.float32, -s(D_MODEL), s(D_MODEL))
        gb = jax.random.uniform(ks[10], (E_ROUTER,), jnp.float32, -s(D_MODEL), s(D_MODEL))
        return {'x': x, 'sW1': sW1, 'sb1': sb1, 'sW2': sW2, 'sb2': sb2, 'rW1': rW1, 'rb1': rb1, 'rW2': rW2, 'rb2': rb2, 'gW': gW, 'gb': gb}
    _L1_ffn_in = _L1_ffn_setup()
    _d = {'L0_attn_x': _L0_attn_in['x'], 'L0_attn_time_maa_x': _L0_attn_in['time_maa_x'], 'L0_attn_time_maa_w': _L0_attn_in['time_maa_w'], 'L0_attn_time_maa_k': _L0_attn_in['time_maa_k'], 'L0_attn_time_maa_v': _L0_attn_in['time_maa_v'], 'L0_attn_time_maa_r': _L0_attn_in['time_maa_r'], 'L0_attn_time_maa_g': _L0_attn_in['time_maa_g'], 'L0_attn_time_maa_w1': _L0_attn_in['time_maa_w1'], 'L0_attn_time_maa_w2': _L0_attn_in['time_maa_w2'], 'L0_attn_time_decay': _L0_attn_in['time_decay'], 'L0_attn_time_decay_w1': _L0_attn_in['time_decay_w1'], 'L0_attn_time_decay_w2': _L0_attn_in['time_decay_w2'], 'L0_attn_W_r': _L0_attn_in['W_r'], 'L0_attn_W_k': _L0_attn_in['W_k'], 'L0_attn_W_v': _L0_attn_in['W_v'], 'L0_attn_W_g': _L0_attn_in['W_g'], 'L0_attn_W_o': _L0_attn_in['W_o'], 'L0_attn_ln_w': _L0_attn_in['ln_w'], 'L0_attn_ln_b': _L0_attn_in['ln_b'], 'L0_ffn_W_fc': _L0_ffn_in['W_fc'], 'L0_ffn_ln_w': _L0_ffn_in['ln_w'], 'L0_ffn_ln_b': _L0_ffn_in['ln_b'], 'L0_ffn_W_proj': _L0_ffn_in['W_proj'], 'L1_attn_W_qkv': _L1_attn_in['W_qkv'], 'L1_attn_W_o': _L1_attn_in['W_o'], 'L1_ffn_sW1': _L1_ffn_in['sW1'], 'L1_ffn_sb1': _L1_ffn_in['sb1'], 'L1_ffn_sW2': _L1_ffn_in['sW2'], 'L1_ffn_sb2': _L1_ffn_in['sb2'], 'L1_ffn_rW1': _L1_ffn_in['rW1'], 'L1_ffn_rb1': _L1_ffn_in['rb1'], 'L1_ffn_rW2': _L1_ffn_in['rW2'], 'L1_ffn_rb2': _L1_ffn_in['rb2'], 'L1_ffn_gW': _L1_ffn_in['gW'], 'L1_ffn_gb': _L1_ffn_in['gb']}
    _x0 = _d['L0_attn_x']
    _d['L0_attn_x'] = jax.random.normal(jax.random.fold_in(jax.random.key(seed), 1), (2, 1024, 128), dtype=_x0.dtype)
    del _x0
    return _d

def reference(L0_attn_x, L0_attn_time_maa_x, L0_attn_time_maa_w, L0_attn_time_maa_k, L0_attn_time_maa_v, L0_attn_time_maa_r, L0_attn_time_maa_g, L0_attn_time_maa_w1, L0_attn_time_maa_w2, L0_attn_time_decay, L0_attn_time_decay_w1, L0_attn_time_decay_w2, L0_attn_W_r, L0_attn_W_k, L0_attn_W_v, L0_attn_W_g, L0_attn_W_o, L0_attn_ln_w, L0_attn_ln_b, L0_ffn_W_fc, L0_ffn_ln_w, L0_ffn_ln_b, L0_ffn_W_proj, L1_attn_W_qkv, L1_attn_W_o, L1_ffn_sW1, L1_ffn_sb1, L1_ffn_sW2, L1_ffn_sb2, L1_ffn_rW1, L1_ffn_rb1, L1_ffn_rW2, L1_ffn_rb2, L1_ffn_gW, L1_ffn_gb):

    def _L0_attn_ref(x, time_maa_x, time_maa_w, time_maa_k, time_maa_v, time_maa_r, time_maa_g, time_maa_w1, time_maa_w2, time_decay, time_decay_w1, time_decay_w2, W_r, W_k, W_v, W_g, W_o, ln_w, ln_b):
        import jax, jax.numpy as jnp
        import numpy as np
        D = 128
        H = 16
        K = 64
        B = 4
        T = 128
        LAYER_ID = 12
        NUM_LAYERS = 24
        D_MIX = 32
        D_DECAY = 64

        def _bidir_shift(x):
            left = jnp.pad(x[:, :-1, :], ((0, 0), (1, 0), (0, 0)))
            right = jnp.pad(x[:, 1:, :], ((0, 0), (0, 1), (0, 0)))
            return 0.5 * (left + right)

        def _lion_attention(r, k, v, w):
            Tn = r.shape[2]
            cs = jnp.cumsum(w, axis=2)
            cs_b = cs - w
            shift_f = cs[:, :, Tn // 2:Tn // 2 + 1, :]
            shift_b = cs_b[:, :, Tn // 2:Tn // 2 + 1, :]
            cf = jnp.clip(cs - shift_f, -60.0, 60.0)
            cb = jnp.clip(cs_b - shift_b, -60.0, 60.0)
            A_f = jnp.einsum('bhik,bhjk->bhij', r * jnp.exp(cf), k * jnp.exp(-cf))
            A_b = jnp.einsum('bhik,bhjk->bhij', r * jnp.exp(-cb), k * jnp.exp(cb))
            idx = jnp.arange(Tn)
            lower = idx[:, None] >= idx[None, :]
            A = jnp.where(lower, A_f, A_b)
            return jnp.einsum('bhij,bhjk->bhik', A, v)
        Bn, Tn, Dn = x.shape
        Hh, Kk = (H, Dn // H)
        dxprev = _bidir_shift(x) - x
        xxx = jnp.tanh((x + dxprev * time_maa_x) @ time_maa_w1)
        mm = jnp.einsum('btfm,fmd->fbtd', xxx.reshape(Bn, Tn, 5, D_MIX), time_maa_w2)
        mw, mk, mv, mr, mg = (mm[0], mm[1], mm[2], mm[3], mm[4])
        xw = x + dxprev * (time_maa_w + mw)
        xk = x + dxprev * (time_maa_k + mk)
        xv = x + dxprev * (time_maa_v + mv)
        xr = x + dxprev * (time_maa_r + mr)
        xg = x + dxprev * (time_maa_g + mg)
        r = xr @ W_r.T
        k = xk @ W_k.T
        v = xv @ W_v.T
        g = jax.nn.silu(xg @ W_g.T)
        w = time_decay + jnp.tanh(xw @ time_decay_w1) @ time_decay_w2
        to_h = lambda t: t.reshape(Bn, Tn, Hh, Kk).transpose(0, 2, 1, 3)
        y = _lion_attention(to_h(r), to_h(k), to_h(v), -jnp.exp(to_h(w)))
        y = y.transpose(0, 2, 1, 3).reshape(Bn * Tn, Dn)
        eps = 1e-05 * 64.0
        yg = y.reshape(Bn * Tn, Hh, Kk)
        mu = jnp.mean(yg, axis=-1, keepdims=True)
        var = jnp.var(yg, axis=-1, keepdims=True)
        yn = ((yg - mu) * jax.lax.rsqrt(var + eps)).reshape(Bn * Tn, Dn) * ln_w + ln_b
        y = yn.reshape(Bn, Tn, Dn)
        return y * g @ W_o.T

    def _L0_ffn_ref(x, W_fc, ln_w, ln_b, W_proj):
        import jax, jax.numpy as jnp
        import numpy as np
        EPS = 1e-06
        LN_EPS = 1e-05

        def _absmean_core(W):
            gamma = jnp.mean(jnp.abs(W)) + EPS
            Ws = W / gamma
            Wq = jnp.sign(Ws) * jnp.minimum(jnp.round(jnp.abs(Ws)), 1.0)
            return (Wq, gamma)

        @jax.custom_vjp
        def absmean(W):
            return _absmean_core(W)[0]

        def _absmean_fwd(W):
            Wq, gamma = _absmean_core(W)
            return (Wq, gamma)

        def _absmean_bwd(gamma, g):
            return (g / gamma,)
        absmean.defvjp(_absmean_fwd, _absmean_bwd)

        def layernorm(x, w, b, eps=LN_EPS):
            mu = jnp.mean(x, axis=-1, keepdims=True)
            var = jnp.mean((x - mu) ** 2, axis=-1, keepdims=True)
            return (x - mu) * jax.lax.rsqrt(var + eps) * w + b
        h = jnp.einsum('btd,hd->bth', x, absmean(W_fc))
        h = jax.nn.gelu(h, approximate=False)
        h = layernorm(h, ln_w, ln_b)
        return jnp.einsum('bth,dh->btd', h, absmean(W_proj))

    def _L1_attn_ref(x, W_qkv, W_o):
        import jax, jax.numpy as jnp
        import numpy as np
        from math import sqrt
        ROPE_BASE = 6000.0

        def _rope_tables(seq_len, rope_dim, dtype):
            inv_freq = 1.0 / ROPE_BASE ** (jnp.arange(0, rope_dim, 2, dtype=jnp.float32) / rope_dim)
            t = jnp.arange(seq_len, dtype=jnp.float32)
            freqs = jnp.outer(t, inv_freq)
            emb = jnp.concatenate([freqs, freqs], axis=-1)
            return (jnp.cos(emb).astype(dtype), jnp.sin(emb).astype(dtype))

        def _rotate_half(x):
            x1, x2 = jnp.split(x, 2, axis=-1)
            return jnp.concatenate([-x2, x1], axis=-1)
        B, S, D = x.shape
        _, H, DK, _ = W_qkv.shape
        rope_dim = DK // 2
        qkv = jnp.einsum('bsm,qhdm->bqhsd', x, W_qkv)
        cos, sin = _rope_tables(S, rope_dim, x.dtype)
        qk = qkv[:, :2, :, :, :rope_dim]
        qk_rot = qk * cos + _rotate_half(qk) * sin
        qkv = qkv.at[:, :2, :, :, :rope_dim].set(qk_rot)
        Q, K, V = (qkv[:, 0], qkv[:, 1], qkv[:, 2])
        scores = jnp.einsum('bhqd,bhkd->bhqk', Q, K)
        causal = jnp.triu(jnp.ones((S, S), dtype=bool), k=1)
        scores = jnp.where(causal, -jnp.inf, scores) / sqrt(DK)
        attn = jax.nn.softmax(scores, axis=-1)
        out = jnp.einsum('bhqk,bhkd->bhqd', attn, V)
        out = out.transpose(0, 2, 1, 3).reshape(B, S, H * DK)
        return jnp.einsum('bsh,dh->bsd', out, W_o)

    def _L1_ffn_ref(x, sW1, sb1, sW2, sb2, rW1, rb1, rW2, rb2, gW, gb):
        import jax, jax.numpy as jnp
        import numpy as np
        D_MODEL = 128
        D_FF = 512
        NUM_M = 2
        E_ROUTER = 8 * NUM_M - 1
        D_FF_R = D_FF // NUM_M
        TOP_K = NUM_M * 2 - 1
        B, T = (2, 256)

        def _expert_stack(x, W1, b1, W2, b2):
            h = jax.nn.gelu(jnp.einsum('btd,edf->ebtf', x, W1) + b1[:, None, None, :], approximate=False)
            return jnp.einsum('ebtf,efd->ebtd', h, W2) + b2[:, None, None, :]
        shared_enc = _expert_stack(x, sW1, sb1, sW2, sb2).sum(0)
        weights = jax.nn.softmax(x @ gW + gb, axis=-1)
        topv, topi = jax.lax.top_k(weights, TOP_K)
        gated = (jax.nn.one_hot(topi, E_ROUTER, dtype=weights.dtype) * topv[..., None]).sum(axis=-2)
        router_out = _expert_stack(x, rW1, rb1, rW2, rb2)
        router_enc = jnp.einsum('ebtd,bte->btd', router_out, gated)
        return shared_enc + router_enc + x
    x = L0_attn_x
    x = x + 0.5 * _L0_ffn_ref(_layernorm(x, axis=-1), L0_ffn_W_fc, L0_ffn_ln_w, L0_ffn_ln_b, L0_ffn_W_proj)
    x = x + _L0_attn_ref(_layernorm(x, axis=-1), L0_attn_time_maa_x, L0_attn_time_maa_w, L0_attn_time_maa_k, L0_attn_time_maa_v, L0_attn_time_maa_r, L0_attn_time_maa_g, L0_attn_time_maa_w1, L0_attn_time_maa_w2, L0_attn_time_decay, L0_attn_time_decay_w1, L0_attn_time_decay_w2, L0_attn_W_r, L0_attn_W_k, L0_attn_W_v, L0_attn_W_g, L0_attn_W_o, L0_attn_ln_w, L0_attn_ln_b)
    x = x + 0.5 * _L0_ffn_ref(_layernorm(x, axis=-1), L0_ffn_W_fc, L0_ffn_ln_w, L0_ffn_ln_b, L0_ffn_W_proj)
    x = x + 0.5 * _L1_ffn_ref(_layernorm(x, axis=-1), L1_ffn_sW1, L1_ffn_sb1, L1_ffn_sW2, L1_ffn_sb2, L1_ffn_rW1, L1_ffn_rb1, L1_ffn_rW2, L1_ffn_rb2, L1_ffn_gW, L1_ffn_gb)
    x = x + _L1_attn_ref(_layernorm(x, axis=-1), L1_attn_W_qkv, L1_attn_W_o)
    x = x + 0.5 * _L1_ffn_ref(_layernorm(x, axis=-1), L1_ffn_sW1, L1_ffn_sb1, L1_ffn_sW2, L1_ffn_sb2, L1_ffn_rW1, L1_ffn_rb1, L1_ffn_rW2, L1_ffn_rb2, L1_ffn_gW, L1_ffn_gb)
    return x

_drawn_inputs = setup_inputs


def setup_inputs(seed=0):
    import zlib

    import numpy as np

    out = dict(_drawn_inputs(seed))
    spreads = {'L0_attn_ln_w': (1.0, 0.6),
     'L0_attn_ln_b': (0.0, 0.8),
     'L0_ffn_ln_w': (1.0, 0.2),
     'L0_ffn_ln_b': (0.0, 0.1)}
    factors = {'L0_attn_time_maa_x': 8.0,
     'L0_attn_time_maa_w': 64.0,
     'L0_attn_time_maa_k': 8.0,
     'L0_attn_time_maa_v': 8.0,
     'L0_attn_time_maa_r': 8.0,
     'L0_attn_time_maa_g': 8.0,
     'L0_attn_time_maa_w1': 8.0,
     'L0_attn_time_maa_w2': 8.0,
     'L0_attn_time_decay': 36.197,
     'L0_attn_time_decay_w1': 64.0,
     'L0_attn_time_decay_w2': 64.0,
     'L0_attn_W_r': 8.0,
     'L0_attn_W_k': 8.0,
     'L0_attn_W_v': 8.0,
     'L0_attn_W_g': 8.0,
     'L0_attn_W_o': 8.0,
     'L1_attn_W_qkv': 8.0,
     'L1_attn_W_o': 8.0,
     'L1_ffn_sW1': 4.588,
     'L1_ffn_sb1': 8.0,
     'L1_ffn_sW2': 4.247,
     'L1_ffn_sb2': 39.712,
     'L1_ffn_rW1': 8.0,
     'L1_ffn_rb1': 8.0,
     'L1_ffn_rW2': 8.0,
     'L1_ffn_rb2': 37.265,
     'L1_ffn_gW': 8.0,
     'L1_ffn_gb': 8.0}
    for name, (base, spread) in spreads.items():
        noise = np.random.default_rng([zlib.crc32(name.encode()), seed]).standard_normal(out[name].shape)
        drawn = base * np.exp(spread * noise) if base else spread * noise
        out[name] = jnp.asarray(drawn.astype(out[name].dtype))
    for name, factor in factors.items():
        out[name] = (out[name] * factor).astype(out[name].dtype)
    return out
```

```python
from contextlib import ExitStack

import concourse.bass as bass
from concourse import mybir

ALU = mybir.AluOpType
ACT = mybir.ActivationFunctionType
F32 = mybir.dt.float32
BF16 = mybir.dt.bfloat16
U8 = mybir.dt.uint8
AX_X = mybir.AxisListType.X

P = 128
D = 128
B = 2
T = 1024
NT = B * T // P
NC = B * T // 512
TPC = 512 // P
LN_EPS = 1e-5


class Store:
    pass


def free(ap):
    return ap.rearrange("p a b -> p (a b)")


def token_tile(xT, t):
    per = T // P
    return xT[:, t // per, 1 + P * (t % per):1 + P * (t % per + 1)]


def token_chunk(xT, k):
    per = T // 512
    return xT[:, k // per, 1 + 512 * (k % per):1 + 512 * (k % per + 1)]


def layernorm_phase(nc, s, tag):
    with ExitStack() as ctx:
        def sem(name):
            return s.semaphores.enter_context(nc.semaphore(f"{tag}_{name}"))

        stats = ctx.enter_context(nc.sbuf_tensor(f"{tag}_stats", [P, NT, 6], F32))
        moments = ctx.enter_context(nc.sbuf_tensor(f"{tag}_moments", [P, NT, 2], F32))
        var_eps = ctx.enter_context(nc.sbuf_tensor(f"{tag}_var_eps", [P, NT], F32))
        std = ctx.enter_context(nc.sbuf_tensor(f"{tag}_std", [P, NT], F32))
        rstd = ctx.enter_context(nc.sbuf_tensor(f"{tag}_rstd", [P, NT], F32))
        turned = ctx.enter_context(nc.psum_tensor(f"{tag}_turned", [P, 4, 512], F32))
        stats_step = sem("stats_step")
        std_done, normed_done = sem("std_done"), sem("normed_done")
        turned_done = sem("turned_done")
        block = ctx.enter_context(nc.Block())

        @block.vector
        def _(dve):
            for t in range(NT):
                dve.bn_stats(stats[:, t, :], s.x[:, t, :]).then_inc(stats_step, 1)
            for t in range(NT):
                dve.wait_ge(stats_step, t + 1)
                dve.bn_aggr(moments[:, t, :], stats[:, t, :]).then_inc(stats_step, 1)
            dve.wait_ge(stats_step, 2 * NT)
            dve.tensor_scalar(var_eps[:, :], moments[:, :, 1], LN_EPS, None, ALU.add).then_inc(stats_step, 1)
            dve.wait_ge(std_done, 1)
            dve.reciprocal(rstd[:, :], std[:, :]).then_inc(stats_step, 1)
            dve.wait_ge(stats_step, 2 * NT + 2)
            for t in range(NT):
                dve.tensor_scalar(s.normed[:, t, :], s.x[:, t, :], moments[:, t, 0:1], rstd[:, t:t + 1],
                                  ALU.subtract, ALU.mult).then_inc(normed_done, 1)

        @block.scalar
        def _(act):
            act.wait_ge(stats_step, 2 * NT + 1)
            act.activation(std[:, :], var_eps[:, :], ACT.Sqrt).then_inc(std_done, 1)
            for k in range(NC):
                act.wait_ge(turned_done, k + 1)
                act.activation(token_chunk(s.xT, k), turned[:, k, :], ACT.Copy)

        @block.tensor
        def _(pe):
            for t in range(NT):
                pe.wait_ge(normed_done, t + 1)
                turn = pe.transpose(turned[:, t // TPC, P * (t % TPC):P * (t % TPC + 1)], s.normed[:, t, :], s.ident[:, :])
                if t % TPC == TPC - 1:
                    turn.then_inc(turned_done, 1)


def load_phase(nc, s, d):
    with ExitStack() as ctx:
        loaded = ctx.enter_context(nc.semaphore("loaded"))
        block = ctx.enter_context(nc.Block())

        @block.sync
        def _(sp):
            sp.dma_start(s.x[:, :, :], d["x"].rearrange("b (n p) c -> p (b n) c", p=P)).then_inc(loaded, 16)
            sp.dma_start(s.ident[:, :], d["eye"]).then_inc(loaded, 16)
            sp.dma_start(s.w_fc[:, :], d["w_fc"]).then_inc(loaded, 16)
            sp.dma_start(s.w_proj[:, :, :], d["w_proj"].rearrange("(n p) c -> p n c", p=P)).then_inc(loaded, 16)
            sp.dma_start(s.ffn_ln[:, :, :], d["ffn_ln"]).then_inc(loaded, 16)
            sp.dma_start(s.gate_w[:, :], d["gate_w"]).then_inc(loaded, 16)
            sp.dma_start(s.gate_b[:, :], d["gate_b"]).then_inc(loaded, 16)
            sp.dma_start(s.expert_b2[:, :], d["expert_b2"]).then_inc(loaded, 16)
            sp.dma_start(s.causal_f[:, :], d["causal"]).then_inc(loaded, 16)
            sp.dma_start(s.rope[:, :, :], d["rope"]).then_inc(s.tables_loaded, 16)
            for to, name in ((s.maa[:, :], "maa"), (s.maa_w1[:, :, :], "maa_w1"), (s.maa_w2[:, :, :], "maa_w2"),
                             (s.mix_w[:, :, :], "mix_w"), (s.decay_w2[:, :], "decay_w2"),
                             (s.decay_w_out[:, :], "decay_w_out"), (s.same_head[:, :], "same_head"),
                             (s.head_of[:, :], "head_of"), (s.key_later_f[:, :], "key_later")):
                sp.dma_start(to, d[name]).then_inc(loaded, 16)
            sp.wait_ge(loaded, 16 * 18)

        @block.vector
        def _(dve):
            dve.memset(s.xT[:, :, :], 0.0)
            dve.wait_ge(loaded, 16 * 18)
            dve.tensor_copy(s.causal[:, :], s.causal_f[:, :])
            dve.tensor_copy(s.key_later[:, :], s.key_later_f[:, :])
            dve.tensor_copy(s.ident_bf[:, :], s.ident[:, :])


def ternary_phase(nc, s):
    with ExitStack() as ctx:
        def sem(name):
            return s.semaphores.enter_context(nc.semaphore(f"tern_{name}"))

        ones = ctx.enter_context(nc.sbuf_tensor("tern_ones", [P, P], F32))
        part = ctx.enter_context(nc.sbuf_tensor("tern_part", [P, 2], F32))
        bound = ctx.enter_context(nc.sbuf_tensor("tern_bound", [P, 4], F32))
        above = ctx.enter_context(nc.sbuf_tensor("tern_above", [P, 2, 512], F32))
        below = ctx.enter_context(nc.sbuf_tensor("tern_below", [P, 2, 512], F32))
        total = ctx.enter_context(nc.psum_tensor("tern_total", [P, 2], F32))
        ones_done, part_done, total_done = sem("ones_done"), sem("part_done"), sem("total_done")
        bound_done, compared = sem("bound_done"), sem("compared")
        block = ctx.enter_context(nc.Block())
        weights = (s.w_fc[:, :], free(s.w_proj[:, :, :]))
        count = float(4 * D * D)

        @block.gpsimd
        def _(pool):
            pool.memset(ones[:, :], 1.0).then_inc(ones_done, 1)

        @block.vector
        def _(dve):
            for n, w in enumerate(weights):
                dve.tensor_reduce(part[:, n:n + 1], w, AX_X, ALU.add, apply_absolute_value=True).then_inc(part_done, 1)
            dve.wait_ge(total_done, 1)
            dve.tensor_scalar(bound[:, 0:2], total[:, :], 1.0 / count, 1e-6, ALU.mult, ALU.add).then_inc(bound_done, 1)
            dve.wait_ge(bound_done, 1)
            dve.tensor_scalar(bound[:, 2:4], bound[:, 0:2], -0.5, None, ALU.mult).then_inc(bound_done, 1)
            dve.wait_ge(bound_done, 2)
            dve.tensor_scalar(bound[:, 0:2], bound[:, 0:2], 0.5, None, ALU.mult).then_inc(bound_done, 1)
            dve.wait_ge(bound_done, 3)
            for n, w in enumerate(weights):
                dve.tensor_scalar(above[:, n, :], w, bound[:, n:n + 1], None, ALU.is_gt).then_inc(compared, 1)
                dve.tensor_scalar(below[:, n, :], w, bound[:, n + 2:n + 3], None, ALU.is_lt).then_inc(compared, 1)
            dve.wait_ge(compared, 4)
            for n, w in enumerate(weights):
                dve.tensor_tensor(w, above[:, n, :], below[:, n, :], ALU.subtract)

        @block.tensor
        def _(pe):
            pe.wait_ge(ones_done, 1)
            pe.wait_ge(part_done, 2)
            pe.matmul(total[:, :], ones[:, :], part[:, :], start=True, stop=True).then_inc(total_done, 1)


def ternary_ffn_phase(nc, s, tag):
    HB = 4
    with ExitStack() as ctx:
        def sem(name):
            return s.semaphores.enter_context(nc.semaphore(f"{tag}_{name}"))

        def sb(name, shape):
            return ctx.enter_context(nc.sbuf_tensor(f"{tag}_{name}", shape, F32))

        def ps(name, shape):
            return ctx.enter_context(nc.psum_tensor(f"{tag}_{name}", shape, F32))

        hidden = sb("hidden", [P, NT, 512])
        hiddenT = sb("hiddenT", [P, HB, NT * P])
        stats, moments = sb("stats", [P, NT, 6]), sb("moments", [P, NT, 2])
        var_eps, std, rstd = sb("var_eps", [P, NT]), sb("std", [P, NT]), sb("rstd", [P, NT])
        up = ps("up", [P, 2, 512])
        turned = ps("turned", [P, 4, 512])
        down = ps("down", [P, 2, 512])
        up_done, gelu_done, stats_step = sem("up_done"), sem("gelu_done"), sem("stats_step")
        std_done = sem("std_done")
        normed_done, turned_done, even_copied, odd_copied = sem("normed_done"), sem("turned_done"), sem("even_copied"), sem("odd_copied")
        down_done, added = sem("down_done"), sem("added")
        block = ctx.enter_context(nc.Block())

        @block.tensor
        def _(pe):
            for t in range(NT):
                if t >= 2:
                    pe.wait_ge(gelu_done, t - 1)
                pe.matmul(up[:, t % 2, :], token_tile(s.xT, t), s.w_fc[:, :], start=True, stop=True).then_inc(up_done, 1)

            def turn_chunk(k):
                pe.wait_ge(normed_done, TPC * (k + 1))
                for hb in range(HB):
                    if k >= 1:
                        copied = even_copied if hb % 2 == 0 else odd_copied
                        pe.wait_ge(copied, 2 * (k - 1) + hb // 2 + 1)
                    for j in range(TPC):
                        turn = pe.transpose(turned[:, hb, P * j:P * j + P],
                                            hidden[:, TPC * k + j, P * hb:P * hb + P], s.ident[:, :])
                    turn.then_inc(turned_done, 1)

            def down_chunk(k):
                pe.wait_ge(even_copied, 2 * (k + 1))
                pe.wait_ge(odd_copied, 2 * (k + 1))
                if k >= 2:
                    pe.wait_ge(added, k - 1)
                for j in range(TPC):
                    for hb in range(HB):
                        at = 512 * k + P * j
                        mm = pe.matmul(down[:, k % 2, P * j:P * j + P], hiddenT[:, hb, at:at + P], s.w_proj[:, hb, :],
                                       start=(hb == 0), stop=(hb == HB - 1))
                mm.then_inc(down_done, 1)

            turn_chunk(0)
            for k in range(NC):
                if k + 1 < NC:
                    turn_chunk(k + 1)
                down_chunk(k)

        @block.scalar
        def _(act):
            for t in range(NT):
                act.wait_ge(up_done, t + 1)
                act.activation(hidden[:, t, :], up[:, t % 2, :], ACT.Gelu).then_inc(gelu_done, 1)
            act.wait_ge(stats_step, 2 * NT + 1)
            act.activation(std[:, :], var_eps[:, :], ACT.Sqrt).then_inc(std_done, 1)
            for k in range(NC):
                for hb in (0, 2):
                    act.wait_ge(turned_done, HB * k + hb + 1)
                    act.activation(hiddenT[:, hb, 512 * k:512 * k + 512], turned[:, hb, :], ACT.Identity,
                                   scale=s.ffn_ln[:, 0, hb:hb + 1], bias=s.ffn_ln[:, 1, hb:hb + 1]).then_inc(even_copied, 1)

        @block.vector
        def _(dve):
            for t in range(NT):
                dve.wait_ge(gelu_done, t + 1)
                dve.bn_stats(stats[:, t, :], hidden[:, t, :]).then_inc(stats_step, 1)
            for t in range(NT):
                dve.wait_ge(stats_step, t + 1)
                dve.bn_aggr(moments[:, t, :], stats[:, t, :]).then_inc(stats_step, 1)
            dve.wait_ge(stats_step, 2 * NT)
            dve.tensor_scalar(var_eps[:, :], moments[:, :, 1], LN_EPS, None, ALU.add).then_inc(stats_step, 1)
            dve.wait_ge(std_done, 1)
            dve.reciprocal(rstd[:, :], std[:, :]).then_inc(stats_step, 1)
            dve.wait_ge(stats_step, 2 * NT + 2)

            def norm_chunk(k):
                for t in range(TPC * k, TPC * k + TPC):
                    dve.tensor_scalar(hidden[:, t, :], hidden[:, t, :], moments[:, t, 0:1], rstd[:, t:t + 1],
                                      ALU.subtract, ALU.mult).then_inc(normed_done, 1)

            norm_chunk(0)
            for k in range(NC):
                if k + 1 < NC:
                    norm_chunk(k + 1)
                for hb in (1, 3):
                    dve.wait_ge(turned_done, HB * k + hb + 1)
                    dve.tensor_scalar(hiddenT[:, hb, 512 * k:512 * k + 512], turned[:, hb, :],
                                      s.ffn_ln[:, 0, hb:hb + 1], s.ffn_ln[:, 1, hb:hb + 1],
                                      ALU.mult, ALU.add).then_inc(odd_copied, 1)
                dve.wait_ge(down_done, k + 1)
                xk = free(s.x[:, TPC * k:TPC * k + TPC, :])
                dve.scalar_tensor_tensor(out=xk, in0=down[:, k % 2, :], scalar=0.5, in1=xk,
                                         op0=ALU.mult, op1=ALU.add).then_inc(added, 1)


def store_phase(nc, s, out):
    with ExitStack() as ctx:
        stored = ctx.enter_context(nc.semaphore("stored"))
        block = ctx.enter_context(nc.Block())

        @block.sync
        def _(sp):
            sp.dma_start(out.rearrange("b (n p) c -> p (b n) c", p=P), s.x[:, :, :]).then_inc(stored, 16)
            sp.wait_ge(stored, 16)


def mix_phase(nc, s, a, tag):
    with ExitStack() as ctx:
        def sem(name):
            return s.semaphores.enter_context(nc.semaphore(f"{tag}_{name}"))

        def sb(name, shape, dt=F32):
            return ctx.enter_context(nc.sbuf_tensor(f"{tag}_{name}", shape, dt))

        def ps(name, shape):
            return ctx.enter_context(nc.psum_tensor(f"{tag}_{name}", shape, F32))

        F = 5
        N = F * NC
        dx, xx = sb("dx", [P, B, T]), sb("xx", [P, B, T])
        low = sb("low", [P, 2, B * T])
        part = sb("part", [P, 2, 512])
        mixed = sb("mixed", [P, 3, 512])
        decay_low = sb("decay_low", [P, B * T])
        mm_bank, proj_bank, decay_bank = ps("mm", [P, 2, 512]), ps("proj", [P, 2, 512]), ps("decay", [P, 2, 512])
        shift_step, low_done, low_copied = sem("shift_step"), sem("low_done"), sem("low_copied")
        mm_done, part_done, mixed_done, proj_done, proj_copied = (sem("mm_done"), sem("part_done"), sem("mixed_done"),
                                                                  sem("proj_done"), sem("proj_copied"))
        decay_done, decay_copied = sem("decay_done"), sem("decay_copied")
        block = ctx.enter_context(nc.Block())

        def flat(ap, k):
            return ap[:, 512 * k:512 * k + 512]

        def chunk(ap, k):
            return ap[:, k // 2, 512 * (k % 2):512 * (k % 2) + 512]

        @block.vector
        def _(dve):
            middle = s.xT[:, :, 1:T + 1]
            dve.tensor_tensor(xx[:, :, :], s.xT[:, :, 0:T], s.xT[:, :, 2:T + 2], ALU.add).then_inc(shift_step, 1)
            dve.wait_ge(shift_step, 1)
            dve.scalar_tensor_tensor(out=dx[:, :, :], in0=xx[:, :, :], scalar=0.5, in1=middle,
                                     op0=ALU.mult, op1=ALU.subtract).then_inc(shift_step, 1)
            dve.wait_ge(shift_step, 2)
            dve.scalar_tensor_tensor(out=xx[:, :, :], in0=dx[:, :, :], scalar=s.maa[:, F:F + 1], in1=middle,
                                     op0=ALU.mult, op1=ALU.add).then_inc(shift_step, 1)
            for n in range(N):
                f, k = n // NC, n % NC
                dve.wait_ge(mm_done, n + 1)
                if n >= 2:
                    dve.wait_ge(mixed_done, n - 1)
                dve.scalar_tensor_tensor(out=part[:, n % 2, :], in0=mm_bank[:, n % 2, :], scalar=s.maa[:, f:f + 1],
                                         in1=chunk(dx, k), op0=ALU.add, op1=ALU.mult).then_inc(part_done, 1)

        @block.gpsimd
        def _(pool):
            for n in range(N):
                pool.wait_ge(part_done, n + 1)
                if n >= 3:
                    pool.wait_ge(proj_done, n - 2)
                pool.tensor_tensor(mixed[:, n % 3, :], part[:, n % 2, :], token_chunk(s.xT, n % NC), ALU.add)\
                    .then_inc(mixed_done, 1)

        @block.tensor
        def _(pe):
            pe.wait_ge(shift_step, 3)
            for n in range(2 * NC):
                k, half = n // 2, n % 2
                if n >= 2:
                    pe.wait_ge(low_copied, n - 1)
                pe.matmul(proj_bank[:, half, :], s.maa_w1[:, half, :], chunk(xx, k), start=True, stop=True)\
                  .then_inc(low_done, 1)

            def project(n):
                f = n // NC
                pe.wait_ge(mixed_done, n + 1)
                if n < 2:
                    pe.wait_ge(low_copied, 2 * NC - 1 + n)
                else:
                    pe.wait_ge(proj_copied, n - 1)
                if f == 2:
                    for j in range(TPC):
                        mm = pe.matmul(proj_bank[:, n % 2, P * j:P * j + P], mixed[:, n % 3, P * j:P * j + P],
                                       s.mix_w[:, f, :], start=True, stop=True)
                else:
                    mm = pe.matmul(proj_bank[:, n % 2, :], s.mix_w[:, f, :], mixed[:, n % 3, :], start=True, stop=True)
                mm.then_inc(proj_done, 1)

            for n in range(N + 2):
                if n < N:
                    f, k = n // NC, n % NC
                    if n < NC:
                        pe.wait_ge(low_copied, 2 * (k + 1))
                    if n >= 2:
                        pe.wait_ge(part_done, n - 1)
                    pe.matmul(mm_bank[:, n % 2, :], s.maa_w2[:, f, :], flat(low[:, f // 4, :], k), start=True, stop=True)\
                      .then_inc(mm_done, 1)
                if n >= 2:
                    project(n - 2)
                if n >= 8 and n - 8 < NC:
                    k = n - 8
                    pe.wait_ge(proj_copied, k + 1)
                    if k >= 2:
                        pe.wait_ge(decay_copied, k - 1)
                    pe.matmul(decay_bank[:, k % 2, :], s.decay_w2[:, :], flat(decay_low, k), start=True, stop=True)\
                      .then_inc(decay_done, 1)

        @block.scalar
        def _(act):
            for n in range(2 * NC):
                act.wait_ge(low_done, n + 1)
                act.activation(flat(low[:, n % 2, :], n // 2), proj_bank[:, n % 2, :], ACT.Tanh).then_inc(low_copied, 1)
            for n in range(N):
                f, k = n // NC, n % NC
                act.wait_ge(proj_done, n + 1)
                to, func = ((flat(decay_low, k), ACT.Tanh), (flat(a.k, k), ACT.Copy), (flat(free(a.v[:, :, :]), k), ACT.Copy),
                            (flat(a.r, k), ACT.Copy), (flat(a.g, k), ACT.Silu))[f]
                act.activation(to, proj_bank[:, n % 2, :], func).then_inc(proj_copied, 1)
                if NC + 2 <= n < 2 * NC + 2:
                    k = n - NC - 2
                    act.wait_ge(decay_done, k + 1)
                    act.activation(flat(a.rate, k), decay_bank[:, k % 2, :], ACT.Exp, bias=s.maa[:, 6:7])\
                       .then_inc(decay_copied, 1)


def decay_phase(nc, s, a, tag):
    with ExitStack() as ctx:
        def sem(name):
            return s.semaphores.enter_context(nc.semaphore(f"{tag}_{name}"))

        zeros = ctx.enter_context(nc.sbuf_tensor(f"{tag}_zeros", [P, T], F32))
        run = ctx.enter_context(nc.sbuf_tensor(f"{tag}_run", [P, 2, B, T], F32))
        clip = ctx.enter_context(nc.sbuf_tensor(f"{tag}_clip", [P, 2, B, T], F32))
        zeroed, run_step, lowered, clipped, grown = sem("zeroed"), sem("run_step"), sem("lowered"), sem("clipped"), sem("grown")
        block = ctx.enter_context(nc.Block())
        MID = T // 2
        FWD, BWD = 0, 1
        FACTORS = ((a.qf, FWD, 1.0, a.r), (a.kf, FWD, -1.0, a.k), (a.qb, BWD, -1.0, a.r), (a.kb, BWD, 1.0, a.k))

        def of(ap, b):
            return ap[:, T * b:T * b + T]

        @block.gpsimd
        def _(pool):
            pool.memset(zeros[:, :], 0.0).then_inc(zeroed, 1)
            for b in range(B):
                for n, (out, way, sign, operand) in enumerate(FACTORS):
                    if n % 2 == 1 and n == 3:
                        pool.wait_ge(grown, 4 * b + n + 1)
                        pool.tensor_tensor(of(out, b), of(out, b), of(operand, b), ALU.mult)

        @block.vector
        def _(dve):
            dve.wait_ge(zeroed, 1)
            for b in range(B):
                dve.tensor_tensor_scan(run[:, FWD, b, :], zeros[:, :], of(a.rate, b), 0.0, ALU.add, ALU.subtract)\
                   .then_inc(run_step, 1)
                dve.wait_ge(run_step, 2 * b + 1)
                dve.tensor_tensor(run[:, BWD, b, :], run[:, FWD, b, :], of(a.rate, b), ALU.add).then_inc(run_step, 1)
                dve.wait_ge(run_step, 2 * b + 2)
                for way in (FWD, BWD):
                    dve.tensor_scalar(clip[:, way, b, :], run[:, way, b, :], run[:, way, b, MID:MID + 1], -60.0,
                                      ALU.subtract, ALU.max).then_inc(lowered, 1)
                for way in (FWD, BWD):
                    dve.wait_ge(lowered, 2 * b + way + 1)
                    dve.tensor_scalar(clip[:, way, b, :], clip[:, way, b, :], 60.0, None, ALU.min).then_inc(clipped, 1)
            for b in range(B):
                for n, (out, way, sign, operand) in enumerate(FACTORS):
                    if n != 3:
                        dve.wait_ge(grown, 4 * b + n + 1)
                        dve.tensor_tensor(of(out, b), of(out, b), of(operand, b), ALU.mult)

        @block.scalar
        def _(act):
            for b in range(B):
                for n, (out, way, sign, operand) in enumerate(FACTORS):
                    act.wait_ge(clipped, 2 * b + way + 1)
                    act.activation(of(out, b), clip[:, way, b, :], ACT.Exp, scale=sign).then_inc(grown, 1)


def state_phase(nc, s, a, tag):
    TB = T // P
    with ExitStack() as ctx:
        def sem(name):
            return s.semaphores.enter_context(nc.semaphore(f"{tag}_{name}"))

        tokens = ctx.enter_context(nc.sbuf_tensor(f"{tag}_tokens", [P, 2, NT, P], F32))
        turned = ctx.enter_context(nc.psum_tensor(f"{tag}_turned", [P, 2, 512], F32))
        outer = ctx.enter_context(nc.psum_tensor(f"{tag}_outer", [P, 4, 512], F32))
        own = ctx.enter_context(nc.sbuf_tensor(f"{tag}_own", [P, 2, NT, P], F32))
        turned_done, tokens_done, outer_done, own_done, summed = (sem("turned_done"), sem("tokens_done"), sem("outer_done"),
                                                                  sem("own_done"), sem("summed"))
        block = ctx.enter_context(nc.Block())
        GROUPS = [(way, k) for k in range(NC) for way in range(2)]

        @block.tensor
        def _(pe):
            for n in range(len(GROUPS) + 1):
                if n < len(GROUPS):
                    way, k = GROUPS[n]
                    keys = a.kf if way == 0 else a.kb
                    if n >= 2:
                        pe.wait_ge(tokens_done, n - 1)
                    for j in range(TPC):
                        at = 512 * k + P * j
                        mm = pe.transpose(turned[:, n % 2, P * j:P * j + P], keys[:, at:at + P], s.ident[:, :])
                    mm.then_inc(turned_done, 1)
                if n >= 1:
                    way, k = GROUPS[n - 1]
                    pe.wait_ge(tokens_done, n)
                    if n - 1 >= 4:
                        pe.wait_ge(own_done, n - 4)
                    for j in range(TPC):
                        t = TPC * k + j
                        mm = pe.matmul(outer[:, (n - 1) % 4, P * j:P * j + P], tokens[:, way, t, :], a.v[:, t, :],
                                       start=True, stop=True)
                    mm.then_inc(outer_done, 1)

        @block.scalar
        def _(act):
            for n, (way, k) in enumerate(GROUPS):
                act.wait_ge(turned_done, n + 1)
                act.activation(free(tokens[:, way, TPC * k:TPC * k + TPC, :]), turned[:, n % 2, :], ACT.Copy)\
                   .then_inc(tokens_done, 1)

        @block.vector
        def _(dve):
            same_head = s.same_head[:, :].unsqueeze(1).to_broadcast([P, TPC, P])
            for n, (way, k) in enumerate(GROUPS):
                dve.wait_ge(outer_done, n + 1)
                dve.tensor_tensor(own[:, way, TPC * k:TPC * k + TPC, :],
                                  outer[:, n % 4, :].rearrange("p (t c) -> p t c", t=TPC), same_head, ALU.mult)\
                   .then_inc(own_done, 1)

        @block.gpsimd
        def _(pool):
            pool.wait_ge(own_done, len(GROUPS))
            for n in range(1, TB):
                for way in range(2):
                    c = n if way == 0 else TB - 1 - n
                    last = c - 1 if way == 0 else c + 1
                    to, mine, held = a.state[:, way, c::TB, :], own[:, way, last::TB, :], a.state[:, way, last::TB, :]
                    if n == 1:
                        pool.tensor_copy(to, mine).then_inc(summed, 1)
                    else:
                        pool.wait_ge(summed, 2 * (n - 1))
                        pool.tensor_tensor(to, mine, held, ALU.add).then_inc(summed, 1)


def chunk_phase(nc, s, a, tag):
    H, K, HQ = 16, 8, 4
    TB = T // P
    with ExitStack() as ctx:
        def sem(name):
            return s.semaphores.enter_context(nc.semaphore(f"{tag}_{name}"))

        per_head = ctx.enter_context(nc.sbuf_tensor(f"{tag}_per_head", [P, 2, 2, H, P], F32))
        score = ctx.enter_context(nc.sbuf_tensor(f"{tag}_score", [P, 4, HQ, P], F32))
        fwd = ctx.enter_context(nc.psum_tensor(f"{tag}_fwd", [P, 2, 512], F32))
        bwd = ctx.enter_context(nc.psum_tensor(f"{tag}_bwd", [P, 2, 512], F32))
        y = ctx.enter_context(nc.psum_tensor(f"{tag}_y", [P, 2, 512], F32))
        fwd_spread, bwd_spread, scored, copied, merged, y_done, y_copied = (
            sem("fwd_spread"), sem("bwd_spread"), sem("scored"), sem("copied"), sem("merged"), sem("y_done"), sem("y_copied"))
        block = ctx.enter_context(nc.Block())
        G = H // HQ

        def spread(eng, t, way):
            src = (a.qf if way == 0 else a.qb)[:, P * t:P * t + P]
            return eng.tensor_tensor(per_head[:, t % 2, way, :, :], src.unsqueeze(1).to_broadcast([P, H, P]),
                                     s.head_of[:, :].unsqueeze(2).to_broadcast([P, H, P]), ALU.mult)

        @block.gpsimd
        def _(pool):
            for t in range(NT):
                if t >= 2:
                    pool.wait_ge(scored, G * (t - 1))
                spread(pool, t, 1).then_inc(bwd_spread, 1)

        @block.tensor
        def _(pe):
            def scores(n):
                t, g = n // G, n % G
                if g == 0:
                    pe.wait_ge(fwd_spread, t + 1)
                    pe.wait_ge(bwd_spread, t + 1)
                if n >= 2:
                    pe.wait_ge(copied, n - 1)
                    pe.wait_ge(merged, n - 1)
                at = slice(P * t, P * t + P)
                pe.matmul(fwd[:, n % 2, :], a.kf[:, at], free(per_head[:, t % 2, 0, HQ * g:HQ * g + HQ, :]), start=True, stop=True)
                pe.matmul(bwd[:, n % 2, :], a.kb[:, at], free(per_head[:, t % 2, 1, HQ * g:HQ * g + HQ, :]), start=True, stop=True)\
                  .then_inc(scored, 1)

            def values(n):
                t, g = n // G, n % G
                at = slice(P * t, P * t + P)
                if g == 0:
                    if t >= 2:
                        pe.wait_ge(y_copied, t - 1)
                    first = True
                    for way, q in ((0, a.qf), (1, a.qb)):
                        if t % TB != (0 if way == 0 else TB - 1):
                            pe.matmul(y[:, t % 2, 0:P], q[:, at], a.state[:, way, t, :], start=first, stop=False,
                                      skip_group_check=True)
                            first = False
                pe.wait_ge(merged, n + 1)
                for j in range(HQ):
                    h = HQ * g + j
                    mm = pe.matmul(y[:, t % 2, K * h:K * h + K], score[:, n % 4, j, :], a.v[:, t, K * h:K * h + K],
                                   start=False, stop=(h == H - 1), skip_group_check=True)
                if g == G - 1:
                    mm.then_inc(y_done, 1)

            for n in range(NT * G + 2):
                if n < NT * G:
                    scores(n)
                if n >= 2:
                    values(n - 2)

        @block.scalar
        def _(act):
            for n in range(NT * G):
                act.wait_ge(scored, n + 1)
                if n >= 8:
                    act.wait_ge(y_done, (n - 4) // G)
                act.activation(score[:, n % 4, :, :], fwd[:, n % 2, :].rearrange("p (h i) -> p h i", h=HQ), ACT.Copy)\
                   .then_inc(copied, 1)
                if n % G == G - 1 and n >= 2 * G - 1:
                    t = n // G - 1
                    act.wait_ge(y_done, t + 1)
                    act.activation(a.y[:, t, :], y[:, t % 2, 0:P], ACT.Copy).then_inc(y_copied, 1)
            act.wait_ge(y_done, NT)
            act.activation(a.y[:, NT - 1, :], y[:, (NT - 1) % 2, 0:P], ACT.Copy)

        @block.vector
        def _(dve):
            later = s.key_later[:, :].unsqueeze(1).to_broadcast([P, HQ, P])
            for n in range(NT * G):
                t, g = n // G, n % G
                if n == 0:
                    spread(dve, 0, 0).then_inc(fwd_spread, 1)
                if g == 0 and t + 1 < NT:
                    if t >= 1:
                        dve.wait_ge(scored, G * t)
                    spread(dve, t + 1, 0).then_inc(fwd_spread, 1)
                dve.wait_ge(copied, n + 1)
                dve.copy_predicated(score[:, n % 4, :, :], later,
                                    bwd[:, n % 2, :].rearrange("p (h i) -> p h i", h=HQ)).then_inc(merged, 1)


def group_norm_phase(nc, s, a, tag):
    H, K = 16, 8
    G = NT * H
    with ExitStack() as ctx:
        def sem(name):
            return s.semaphores.enter_context(nc.semaphore(f"{tag}_{name}"))

        def sb(name, shape):
            return ctx.enter_context(nc.sbuf_tensor(f"{tag}_{name}", shape, F32))

        mean, var, std, rstd = sb("mean", [P, G]), sb("var", [P, G]), sb("std", [P, G]), sb("rstd", [P, G])
        square = sb("square", [P, G, K])
        scaled = sb("scaled", [P, 2, 512])
        gated = sb("gated", [P, B * T])
        turned = ctx.enter_context(nc.psum_tensor(f"{tag}_turned", [P, NC, 512], F32))
        mixed = ctx.enter_context(nc.psum_tensor(f"{tag}_mixed", [P, 2, 512], F32))
        step, std_done, turned_done, scaled_done, gated_done = (sem("step"), sem("std_done"), sem("turned_done"),
                                                                sem("scaled_done"), sem("gated_done"))
        mixed_done, added = sem("mixed_done"), sem("added")
        block = ctx.enter_context(nc.Block())
        y = a.y[:, :, :].rearrange("p t (h k) -> p (t h) k", k=K)

        def wide(ap):
            return ap.unsqueeze(2).to_broadcast([P, G, K])

        @block.vector
        def _(dve):
            dve.tensor_reduce(mean[:, :], y, AX_X, ALU.add).then_inc(step, 1)
            dve.wait_ge(step, 1)
            dve.tensor_scalar(mean[:, :], mean[:, :], 1.0 / K, None, ALU.mult).then_inc(step, 1)
            dve.wait_ge(step, 2)
            dve.tensor_tensor(y, y, wide(mean[:, :]), ALU.subtract).then_inc(step, 1)
            dve.wait_ge(step, 3)
            dve.tensor_tensor(square[:, :, :], y, y, ALU.mult).then_inc(step, 1)
            dve.wait_ge(step, 4)
            dve.tensor_reduce(var[:, :], square[:, :, :], AX_X, ALU.add).then_inc(step, 1)
            dve.wait_ge(step, 5)
            dve.tensor_scalar(var[:, :], var[:, :], 1.0 / K, 1e-05 * 64.0, ALU.mult, ALU.add).then_inc(step, 1)
            dve.wait_ge(std_done, 1)
            dve.reciprocal(rstd[:, :], std[:, :]).then_inc(step, 1)
            dve.wait_ge(step, 7)
            dve.tensor_tensor(y, y, wide(rstd[:, :]), ALU.mult).then_inc(step, 1)
            for k in range(NC):
                dve.wait_ge(turned_done, k + 1)
                if k >= 2:
                    dve.wait_ge(gated_done, k - 1)
                dve.tensor_scalar(scaled[:, k % 2, :], turned[:, k, :], s.maa[:, 7:8], s.maa[:, 8:9], ALU.mult, ALU.add)\
                   .then_inc(scaled_done, 1)
            for k in range(NC):
                dve.wait_ge(mixed_done, k + 1)
                xk = free(s.x[:, TPC * k:TPC * k + TPC, :])
                dve.tensor_tensor(xk, mixed[:, k % 2, :], xk, ALU.add).then_inc(added, 1)

        @block.scalar
        def _(act):
            act.wait_ge(step, 6)
            act.activation(std[:, :], var[:, :], ACT.Sqrt).then_inc(std_done, 1)

        @block.gpsimd
        def _(pool):
            for k in range(NC):
                pool.wait_ge(scaled_done, k + 1)
                at = slice(512 * k, 512 * k + 512)
                pool.tensor_tensor(gated[:, at], scaled[:, k % 2, :], a.g[:, at], ALU.mult).then_inc(gated_done, 1)

        @block.tensor
        def _(pe):
            pe.wait_ge(step, 8)
            for t in range(NT):
                turn = pe.transpose(turned[:, t // TPC, P * (t % TPC):P * (t % TPC) + P], a.y[:, t, :], s.ident[:, :])
                if t % TPC == TPC - 1:
                    turn.then_inc(turned_done, 1)
            for k in range(NC):
                pe.wait_ge(gated_done, k + 1)
                if k >= 2:
                    pe.wait_ge(added, k - 1)
                for j in range(TPC):
                    at = 512 * k + P * j
                    mm = pe.matmul(mixed[:, k % 2, P * j:P * j + P], gated[:, at:at + P], s.decay_w_out[:, :],
                                   start=True, stop=True)
                mm.then_inc(mixed_done, 1)


def decay_attention_phase(nc, s, d, tag):
    with ExitStack() as ctx:
        def sb(name, shape):
            return ctx.enter_context(nc.sbuf_tensor(f"{tag}_{name}", shape, F32))

        a = Store()
        a.v, a.g = sb("v", [P, NT, P]), sb("g", [P, B * T])
        a.qf, a.kf, a.qb, a.kb = (sb(n, [P, B * T]) for n in ("qf", "kf", "qb", "kb"))
        with nc.sbuf_tensor(f"{tag}_r", [P, B * T], F32) as a.r, nc.sbuf_tensor(f"{tag}_k", [P, B * T], F32) as a.k, \
                nc.sbuf_tensor(f"{tag}_rate", [P, B * T], F32) as a.rate:
            mix_phase(nc, s, a, f"{tag}_mix")
            decay_phase(nc, s, a, f"{tag}_decay")
        a.state, a.y = sb("state", [P, 2, NT, P]), sb("y", [P, NT, P])
        state_phase(nc, s, a, f"{tag}_state")
        chunk_phase(nc, s, a, f"{tag}_chunk")
        group_norm_phase(nc, s, a, f"{tag}_norm")


def softmax_attention_phase(nc, s, d, tag):
    PAIRS, DK = 8, 64
    TB = T // P
    ORDER = [7, 0, 6, 1, 5, 2, 4, 3]
    STEPS = [(b, i, h) for b in range(B) for i in ORDER for h in range(2)]
    N = len(STEPS)
    NT_BUF = 4
    NP = 8
    BANKS, FREED, bank = [], [], 0
    for n, (b, i, h) in enumerate(STEPS * 2):
        width = i // 4 + 1
        assert bank % 4 + width <= 4
        BANKS.append(bank % 4)
        used = range(bank % 4, bank % 4 + width)
        FREED.append(max([m - N for m in range(n) if any(BANKS[m] <= u <= BANKS[m] + STEPS[m % N][1] // 4 for u in used)],
                         default=None))
        bank += width
    assert BANKS[:N] == BANKS[N:]
    BANKS, FREED = BANKS[:N], FREED[N:]
    QUADS, quad = [], 0
    for b, i, h in STEPS:
        QUADS.append([(quad + z, 4 * z, min(4 * z + 4, i + 1)) for z in range(i // 4 + 1)])
        quad += i // 4 + 1
    NQ = quad
    UNITS = [(kk, kind) for kk in range(2) for kind in range(2)]
    NU = len(UNITS)
    NV = 2
    assert NQ % 2 == 0
    MIX_AT = N // 2 + 3
    NORM_LAG, TURN_LAG, PV_LAG = 2, 4, 5
    JOBS = {}
    for half, rope_at, v_at in ((1, (0, 1, 2, 3), (4, 5)), (2, (27, 29, 31, 32), (33, 34))):
        for u, n in enumerate(rope_at):
            JOBS.setdefault(n, []).append(("rope", half, u))
        for g, n in enumerate(v_at):
            JOBS.setdefault(n, []).append(("v", half, g))
    NJ = NU + NV
    with ExitStack() as ctx:
        def sem(name):
            return s.semaphores.enter_context(nc.semaphore(f"{tag}_{name}"))

        def sb(name, shape, dt=F32):
            return ctx.enter_context(nc.sbuf_tensor(f"{tag}_{name}", shape, dt))

        def ps(name, shape):
            return ctx.enter_context(nc.psum_tensor(f"{tag}_{name}", shape, F32))

        w_in, w_out = sb("w_in", [P, 3, P]), sb("w_out", [P, D])
        q = sb("q", [P, 2, B, T])
        k = sb("k", [P, B, T])
        v = sb("v", [P, NT, P])
        by_cos, by_sin = sb("by_cos", [P, 2, 512]), sb("by_sin", [P, 2, 512])
        prob = sb("prob", [P, NP, T])
        probT = sb("probT", [P, NT_BUF, T])
        headT = sb("headT", [P, NT, P])
        neg_max, total, inverse = sb("neg_max", [P, N]), sb("total", [P, N]), sb("inverse", [P, N])
        score = ps("score", [P, 4 * 512])
        turned = ps("turned", [P, 2, 512])
        projected = ps("projected", [P, 512])
        out = ps("out", [P, 4, P])
        w_in_loaded, w_out_loaded = sem("w_in_loaded"), sem("w_out_loaded")
        projection_copied = sem("projection_copied")
        zeroed, proj_done, v_done, rope_step, rope_done = (sem("zeroed"), sem("proj_done"), sem("v_done"),
                                                           sem("rope_step"), sem("rope_done"))
        score_done, max_done, exp_done, inverse_done, prob_done = (sem("score_done"), sem("max_done"), sem("exp_done"),
                                                                   sem("inverse_done"), sem("prob_done"))
        turned_done, copied, pv_done = sem("turned_done"), [sem("even_copied"), sem("odd_copied")], sem("pv_done")
        head_copied, mixed_done, added = sem("head_copied"), sem("mixed_done"), sem("added")
        EXP0, TURNED0, COPIED0, PV0, HEAD0, ADDED0 = 4, NQ, 1, NT_BUF, 1, 4
        block = ctx.enter_context(nc.Block())

        def jobs_before(p, job):
            kind, half, number = job
            return (p * 2 + half) * NJ + (number if kind == "rope" else NU + number)

        def last_quad(step):
            return QUADS[step][-1][0] + 1

        @block.sync
        def _(sp):
            def load_in(p):
                sp.dma_start(w_in[:, :, :].rearrange("p a b -> p (a b)"),
                             d["attn_in"][bass.ds(p, 1), :, :].rearrange("a p w -> p (a w)")).then_inc(w_in_loaded, 16)

            def load_out(p):
                sp.dma_start(w_out[:, :], d["attn_out"][bass.ds(p, 1), :, :].rearrange("a p w -> p (a w)"))\
                  .then_inc(w_out_loaded, 16)

            load_in(0)
            load_out(0)
            with sp.Fori(0, PAIRS - 1) as p:
                sp.wait_ge(v_done, p * (2 * NV) + 2 * NV)
                sp.wait_ge(w_in_loaded, p * 16 + 16)
                load_in(p + 1)
                sp.wait_ge(mixed_done, p * 4 + 4)
                sp.wait_ge(w_out_loaded, p * 16 + 16)
                load_out(p + 1)
            sp.wait_ge(v_done, PAIRS * 2 * NV)
            sp.wait_ge(w_in_loaded, PAIRS * 16)
            load_in(PAIRS)

        @block.gpsimd
        def _(pool):
            for sm, count in ((exp_done, EXP0), (turned_done, TURNED0), (copied[0], COPIED0), (copied[1], COPIED0), (pv_done, PV0), (head_copied, HEAD0), (added, ADDED0)):
                pool.sem_inc(sm, count)
            pool.memset(q[64:128, 0, :, :], 0.0).then_inc(zeroed, 1)
            pool.memset(q[0:64, 1, :, :], 0.0).then_inc(zeroed, 1)
            pool.wait_ge(s.tables_loaded, 16)

            def rope(p, job):
                _, half, u = job
                kk, kind = UNITS[u]
                b, at = half % 2, slice(512 * kk, 512 * kk + 512)
                H = p * 2 + half
                pool.wait_ge(projection_copied, jobs_before(p, job) + 1)
                pool.tensor_tensor(by_sin[:, u % 2, :], by_sin[:, u % 2, :], s.rope[:, 2 * kind + 1, at], ALU.mult)\
                    .then_inc(rope_step, 1)
                steps = H * 6 + (3 * kk + 2 * kind + 1)
                pool.wait_ge(rope_step, steps)
                if kind == 0:
                    pool.tensor_tensor(q[0:64, 0, b, at], by_cos[0:64, u % 2, :], by_sin[0:64, u % 2, :], ALU.add)\
                        .then_inc(rope_step, 1)
                    pool.wait_ge(rope_step, steps + 1)
                    pool.tensor_tensor(q[64:128, 1, b, at], by_cos[64:128, u % 2, :], by_sin[64:128, u % 2, :], ALU.add)\
                        .then_inc(rope_done, 1)
                    pool.wait_ge(rope_done, H * NU + (u + 1))
                else:
                    pool.tensor_tensor(k[:, b, at], by_cos[:, u % 2, :], by_sin[:, u % 2, :], ALU.add).then_inc(rope_done, 1)

            pool.wait_ge(zeroed, 2)
            for u in range(NU):
                rope(0, ("rope", 0, u))
            with pool.Fori(0, PAIRS) as p:
                for n in range(N + PV_LAG):
                    for job in JOBS.get(n, []):
                        if job[0] == "rope":
                            rope(p, job)

        @block.tensor
        def _(pe):
            def project(p, job):
                kind_of_job, half, number = job
                b, H = half % 2, p * 2 + half
                pe.wait_ge(w_in_loaded, (p + half // 2) * 16 + 16)
                if job != ("rope", 0, 0):
                    pe.wait_ge(projection_copied, jobs_before(p, job))
                if kind_of_job == "rope":
                    kk, kind = UNITS[number]
                    pe.matmul(projected[:, :], w_in[:, kind, :], token_chunk(s.xT, 2 * b + kk), start=True, stop=True)\
                      .then_inc(proj_done, 1)
                else:
                    for j in range(TPC):
                        mm = pe.matmul(projected[:, P * j:P * j + P], token_tile(s.xT, TB * b + TPC * number + j),
                                       w_in[:, 2, :], start=True, stop=True)
                    mm.then_inc(v_done, 1)

            def scores(p, n):
                b, i, h = STEPS[n]
                if n % (N // 2) == 0:
                    pe.wait_ge(rope_done, (p * 2 + b) * NU + NU)
                pe.wait_ge(exp_done, p * N + (FREED[n] + 1 + EXP0))
                cols, base = P * (i + 1), 512 * BANKS[n]
                for at in range(0, cols, 512):
                    upto = min(at + 512, cols)
                    pe.matmul(score[:, base + at:base + upto], q[:, h, b, P * i:P * i + P], k[:, b, at:upto],
                              start=True, stop=(upto < cols), skip_group_check=True)
                pe.matmul(score[:, base + P * i:base + P * i + P], s.ident_bf[:, :], s.causal[:, :], start=False, stop=True,
                          skip_group_check=True).then_inc(score_done, 1)

            def turn(p, n):
                pe.wait_ge(prob_done, p * N + (n + 1))
                for z, lo, hi in QUADS[n]:
                    pe.wait_ge(copied[z % 2], p * (NQ // 2) + (z // 2 + COPIED0))
                    for kb in range(lo, hi):
                        mm = pe.transpose(turned[:, z % 2, P * (kb - lo):P * (kb - lo) + P],
                                          prob[:, n % NP, P * kb:P * kb + P], s.ident[:, :])
                    mm.then_inc(turned_done, 1)

            def times_v(p, n):
                b, i, h = STEPS[n]
                m = n // 2
                if n % (N // 2) == 0:
                    pe.wait_ge(projection_copied, (p * 2 + b) * NJ + NJ)
                if h == 0:
                    pe.wait_ge(head_copied, p * (N // 2) + (m + HEAD0))
                    if m == 0:
                        pe.wait_ge(added, p * 4 + ADDED0)
                    elif m == (MIX_AT + 1) // 2:
                        pe.wait_ge(added, p * 4 + (2 + ADDED0))
                for z, lo, hi in QUADS[n]:
                    pe.wait_ge(copied[z % 2], p * (NQ // 2) + (z // 2 + 1 + COPIED0))
                    for kb in range(lo, hi):
                        mm = pe.matmul(out[DK * h:DK * h + DK, m % 4, :], v[:, TB * b + kb, DK * h:DK * h + DK],
                                       probT[:, n % NT_BUF, P * kb:P * kb + P], start=(kb == 0), stop=(kb == i))
                mm.then_inc(pv_done, 1)

            def mix(p, b):
                pe.wait_ge(w_out_loaded, p * 16 + 16)
                pe.wait_ge(head_copied, p * (N // 2) + ((N // 2 if b else (MIX_AT + 1) // 2) + HEAD0))
                for g in range(2):
                    pe.wait_ge(added, p * 4 + (2 * b + g + ADDED0))
                    for j in range(TPC):
                        mm = pe.matmul(out[:, j, :], headT[:, TB * b + TPC * g + j, :], w_out[:, :],
                                       start=True, stop=True)
                    mm.then_inc(mixed_done, 1)

            pe.wait_ge(zeroed, 2)
            for u in range(NU):
                project(0, ("rope", 0, u))
            for g in range(NV):
                project(0, ("v", 0, g))
            with pe.Fori(0, PAIRS) as p:
                for n in range(N + PV_LAG):
                    if n < N:
                        scores(p, n)
                    for job in JOBS.get(n, []):
                        project(p, job)
                    if 0 <= n - TURN_LAG < N:
                        turn(p, n - TURN_LAG)
                    if 0 <= n - PV_LAG < N:
                        times_v(p, n - PV_LAG)
                    if n == MIX_AT + PV_LAG:
                        mix(p, 0)
                mix(p, 1)

        def copy_quad(eng, copy, p, n, which):
            for z, lo, hi in QUADS[n]:
                if z % 2 == which:
                    eng.wait_ge(turned_done, p * NQ + (z + 1 + TURNED0))
                    eng.wait_ge(pv_done, p * N + (n - NT_BUF + 1 + PV0))
                    copy(probT[:, n % NT_BUF, P * lo:P * hi], turned[:, which, 0:P * (hi - lo)]).then_inc(copied[which], 1)

        @block.scalar
        def _(act):
            def copy(out, in_):
                return act.activation(out, in_, ACT.Copy)

            def copy_v(p, job):
                _, half, g = job
                at = TB * (half % 2) + TPC * g
                act.wait_ge(v_done, (p * 2 + half) * NV + (g + 1))
                copy(free(v[:, at:at + TPC, :]), projected[:, :]).then_inc(projection_copied, 1)

            for g in range(NV):
                copy_v(0, ("v", 0, g))
            with act.Fori(0, PAIRS) as p:
                for n in range(N + PV_LAG):
                    if n < N:
                        b, i, h = STEPS[n]
                        act.wait_ge(max_done, p * N + (n + 1))
                        before = last_quad(n - NP) + TURNED0 if n >= NP else last_quad(n - NP + N) + TURNED0 - NQ
                        act.wait_ge(turned_done, p * NQ + before)
                        act.activation(prob[:, n % NP, 0:P * (i + 1)], score[:, 512 * BANKS[n]:512 * BANKS[n] + P * (i + 1)], ACT.Exp,
                                       bias=neg_max[:, n:n + 1], accum_out=total[:, n:n + 1]).then_inc(exp_done, 1)
                    for job in JOBS.get(n, []):
                        if job[0] == "v":
                            copy_v(p, job)
                    if 0 <= n - TURN_LAG < N:
                        copy_quad(act, copy, p, n - TURN_LAG, 0)
                    done = n - PV_LAG
                    if done >= 0 and done % 2 == 1:
                        b, i, h = STEPS[done]
                        act.wait_ge(pv_done, p * N + (done + 1 + PV0))
                        copy(headT[:, TB * b + i, :], out[:, done // 2 % 4, :]).then_inc(head_copied, 1)

        @block.vector
        def _(dve):
            def add_mixed(p, b):
                for g in range(2):
                    c = 2 * b + g
                    dve.wait_ge(mixed_done, p * 4 + (c + 1))
                    dve.wait_ge(added, p * 4 + (c + 1))
                    xk = free(s.x[:, TPC * c:TPC * c + TPC, :])
                    dve.tensor_tensor(xk, free(out[:, :, :]), xk, ALU.add).then_inc(added, 1)

            HALVES_SWAPPED = list(range(16, 32)) + list(range(16))

            def rope(p, job):
                _, half, u = job
                kk, kind = UNITS[u]
                unit = (p * 2 + half) * NU + u
                dve.wait_ge(proj_done, unit + 1)
                if half > 0 or u >= 2:
                    dve.wait_ge(rope_done, unit - 1)
                dve.tensor_tensor(by_cos[:, u % 2, :], projected[:, :], s.rope[:, 2 * kind, 512 * kk:512 * kk + 512], ALU.mult)
                dve.stream_shuffle(by_sin[:, u % 2, :], projected[:, :], HALVES_SWAPPED).then_inc(projection_copied, 1)

            dve.wait_ge(s.tables_loaded, 16)
            for u in range(NU):
                rope(0, ("rope", 0, u))
            with dve.Fori(0, PAIRS) as p:
                for n in range(N + PV_LAG):
                    m = n - NORM_LAG
                    if 0 <= m < N:
                        dve.wait_ge(exp_done, p * N + (m + 1 + EXP0))
                        dve.reciprocal(inverse[:, m:m + 1], total[:, m:m + 1]).then_inc(inverse_done, 1)
                        dve.wait_ge(inverse_done, p * N + (m + 1))
                        row = prob[:, m % NP, 0:P * (STEPS[m][1] + 1)]
                        dve.tensor_scalar(row, row, inverse[:, m:m + 1], None, ALU.mult).then_inc(prob_done, 1)
                    if n < N:
                        b, i, h = STEPS[n]
                        dve.wait_ge(score_done, p * N + (n + 1))
                        dve.tensor_reduce(neg_max[:, n:n + 1], score[:, 512 * BANKS[n]:512 * BANKS[n] + P * (i + 1)], AX_X, ALU.max, negate=True)\
                           .then_inc(max_done, 1)
                    for job in JOBS.get(n, []):
                        if job[0] == "rope":
                            rope(p, job)
                    if 0 <= n - TURN_LAG < N:
                        copy_quad(dve, dve.tensor_copy, p, n - TURN_LAG, 1)
                    if n == MIX_AT + PV_LAG:
                        add_mixed(p, 0)
                add_mixed(p, 1)


def expert_ffn_phase(nc, s, d, tag):
    E, R, F, TOP = 17, 15, 256, 3
    S = E - R
    W1, W2 = 2, 2 + F
    ROW = 2 + 2 * F
    with ExitStack() as ctx:
        def sem(name):
            return s.semaphores.enter_context(nc.semaphore(f"{tag}_{name}"))

        def sb(name, shape):
            return ctx.enter_context(nc.sbuf_tensor(f"{tag}_{name}", shape, F32))

        def ps(name, shape):
            return ctx.enter_context(nc.psum_tensor(f"{tag}_{name}", shape, F32))

        weights = sb("weights", [P, 2, ROW])
        hidden = sb("hidden", [P, 2, 2, 512])
        acc = sb("acc", [P, NT, D])
        score, prob = sb("score", [P, NT, R]), sb("prob", [P, NT, R])
        beats, rank = sb("beats", [P, NT, R, R]), sb("rank", [P, NT, R])
        top, total, inverse = sb("top", [P, NT]), sb("total", [P, NT]), sb("inverse", [P, NT])
        gates = sb("gates", [P, E, NT])
        gatesT = sb("gatesT", [P, NT * P])
        up = ps("up", [P, 2, 2, 512])
        down = ps("down", [P, 2, 512])
        side = ps("side", [P, 2, 512])
        w_loaded = [sem("w0_loaded"), sem("w1_loaded")]
        logits_done, gate_step, exp_done, gates_done = sem("logits_done"), sem("gate_step"), sem("exp_done"), sem("gates_done")
        zeroed, turned_done, turned_copied = sem("zeroed"), sem("turned_done"), sem("turned_copied")
        bias_done, bias_added = sem("bias_done"), sem("bias_added")
        up_done, gelu_done, down_done, acc_done = sem("up_done"), sem("gelu_done"), sem("down_done"), sem("acc_done")
        block = ctx.enter_context(nc.Block())
        logits = side[:, 0, 0:NT * R].rearrange("p (t e) -> p t e", e=R)

        @block.sync
        def _(sp):
            def load(e, parity):
                sp.dma_start(weights[:, parity, :], d["experts"][bass.ds(e, 1), :, :].rearrange("a p w -> p (a w)"))\
                  .then_inc(w_loaded[parity], 16)

            load(0, 0)
            load(1, 1)
            with sp.Fori(0, (E - 3) // 2) as i:
                sp.wait_ge(down_done, i * 8 + 4)
                sp.wait_ge(w_loaded[0], i * 16 + 16)
                load(i * 2 + 2, 0)
                sp.wait_ge(down_done, i * 8 + 8)
                sp.wait_ge(w_loaded[1], i * 16 + 16)
                load(i * 2 + 3, 1)
            sp.wait_ge(down_done, 4 * (E - 2))
            sp.wait_ge(w_loaded[0], 16 * (E - 1) // 2)
            load(E - 1, 0)

        @block.gpsimd
        def _(pool):
            pool.memset(gates[:, 0:S, :], 1.0).then_inc(zeroed, 1)
            pool.memset(gatesT[:, :], 0.0).then_inc(zeroed, 1)
            pool.memset(beats[:, :, :, :], 0.0).then_inc(zeroed, 1)

        @block.tensor
        def _(pe):
            for t in range(NT):
                mm = pe.matmul(logits[:, t, :], token_tile(s.xT, t), s.gate_w[:, :], start=True, stop=True)
            mm.then_inc(logits_done, 1)

            def up_chunk(n, k, parity):
                for m in range(2):
                    pe.matmul(up[:, k % 2, m, :], weights[:, parity, W1 + P * m:W1 + P * m + P], token_chunk(s.xT, k),
                              start=True, stop=True).then_inc(up_done, 1)

            def down_chunk(k, parity):
                for j in range(TPC):
                    for m in range(2):
                        mm = pe.matmul(down[:, k % 2, P * j:P * j + P], hidden[:, k % 2, m, P * j:P * j + P],
                                       weights[:, parity, W2 + P * m:W2 + P * m + P], start=(m == 0), stop=(m == 1))
                mm.then_inc(down_done, 1)

            pe.wait_ge(w_loaded[0], 16)
            for k in range(NC):
                if k >= 2:
                    pe.wait_ge(gelu_done, 2 * (k - 1))
                up_chunk(k, k, 0)
                if k >= 1:
                    pe.wait_ge(gelu_done, 2 * k)
                    if k >= 3:
                        pe.wait_ge(acc_done, k - 2)
                    down_chunk(k - 1, 0)
            pe.wait_ge(gates_done, 1)
            pe.wait_ge(zeroed, 3)
            for g in range(NC):
                if g >= 2:
                    pe.wait_ge(turned_copied, g - 1)
                for j in range(TPC):
                    turn = pe.transpose(side[0:E, g % 2, P * j:P * j + P], gates[:, :, TPC * g + j], s.ident[:, :])
                turn.then_inc(turned_done, 1)
            for g in range(NC):
                if g < 2:
                    pe.wait_ge(turned_copied, NC - 1 + g)
                else:
                    pe.wait_ge(bias_added, g - 1)
                for j in range(TPC):
                    at = 512 * g + P * j
                    mm = pe.matmul(side[:, g % 2, P * j:P * j + P], gatesT[:, at:at + P], s.expert_b2[:, :],
                                   start=True, stop=True)
                mm.then_inc(bias_done, 1)
            with pe.Fori(0, (E - 1) // 2) as i:
                for c in range(2 * NC):
                    k = c % NC
                    parity = 1 - c // NC
                    n = i * 8 + (NC + c)
                    if c == 0:
                        pe.wait_ge(w_loaded[1], i * 16 + 16)
                    if c == NC:
                        pe.wait_ge(w_loaded[0], i * 16 + 32)
                    pe.wait_ge(gelu_done, (n - 1) * 2)
                    up_chunk(n, k, parity)
                    pe.wait_ge(gelu_done, n * 2)
                    pe.wait_ge(acc_done, n - 2)
                    down_chunk((k - 1) % NC, parity if k else 1 - parity)
            pe.wait_ge(gelu_done, 2 * E * NC)
            pe.wait_ge(acc_done, E * NC - 2)
            down_chunk(NC - 1, 0)

        @block.scalar
        def _(act):
            def gelu_chunk(n, k, parity):
                for m in range(2):
                    act.wait_ge(up_done, n * 2 + (m + 1))
                    act.activation(hidden[:, k % 2, m, :], up[:, k % 2, m, :], ACT.Gelu,
                                   bias=weights[:, parity, m:m + 1]).then_inc(gelu_done, 1)

            act.wait_ge(gate_step, 3)
            act.activation(prob[:, :, :], score[:, :, :], ACT.Exp).then_inc(exp_done, 1)
            for k in range(NC):
                if k >= 2:
                    act.wait_ge(down_done, k - 1)
                gelu_chunk(k, k, 0)
            for g in range(NC):
                act.wait_ge(turned_done, g + 1)
                act.activation(gatesT[0:E, 512 * g:512 * g + 512], side[0:E, g % 2, :], ACT.Copy).then_inc(turned_copied, 1)
            with act.Fori(0, (E - 1) // 2) as i:
                for c in range(2 * NC):
                    n = i * 8 + (NC + c)
                    act.wait_ge(down_done, n - 1)
                    gelu_chunk(n, c % NC, 1 - c // NC)

        @block.vector
        def _(dve):
            def wide(ap):
                return ap.unsqueeze(2).to_broadcast([P, NT, R])

            def add_bias(g):
                dve.wait_ge(bias_done, g + 1)
                dve.wait_ge(acc_done, g + 1)
                a = free(acc[:, TPC * g:TPC * g + TPC, :])
                dve.tensor_tensor(a, side[:, g % 2, :], a, ALU.add).then_inc(bias_added, 1)

            dve.wait_ge(logits_done, 1)
            dve.tensor_tensor(score[:, :, :], logits, s.gate_b[:, :].unsqueeze(1).to_broadcast([P, NT, R]), ALU.add)\
               .then_inc(gate_step, 1)
            dve.wait_ge(gate_step, 1)
            dve.tensor_reduce(top[:, :], score[:, :, :], AX_X, ALU.max).then_inc(gate_step, 1)
            dve.wait_ge(gate_step, 2)
            dve.tensor_tensor(score[:, :, :], score[:, :, :], wide(top[:, :]), ALU.subtract).then_inc(gate_step, 1)
            dve.wait_ge(exp_done, 1)
            dve.tensor_reduce(total[:, :], prob[:, :, :], AX_X, ALU.add).then_inc(gate_step, 1)
            dve.wait_ge(gate_step, 4)
            dve.reciprocal(inverse[:, :], total[:, :]).then_inc(gate_step, 1)
            dve.wait_ge(gate_step, 5)
            dve.tensor_tensor(prob[:, :, :], prob[:, :, :], wide(inverse[:, :]), ALU.mult).then_inc(gate_step, 1)
            dve.wait_ge(gate_step, 6)
            dve.wait_ge(zeroed, 3)
            for e in range(R):
                if e > 0:
                    dve.tensor_tensor(beats[:, :, e, 0:e], prob[:, :, 0:e],
                                      prob[:, :, e:e + 1].to_broadcast([P, NT, e]), ALU.is_ge).then_inc(gate_step, 1)
                if e < R - 1:
                    dve.tensor_tensor(beats[:, :, e, e + 1:R], prob[:, :, e + 1:R],
                                      prob[:, :, e:e + 1].to_broadcast([P, NT, R - 1 - e]), ALU.is_gt).then_inc(gate_step, 1)
            dve.wait_ge(gate_step, 6 + 2 * (R - 1))
            dve.tensor_reduce(rank[:, :, :], beats[:, :, :, :], AX_X, ALU.add).then_inc(gate_step, 1)
            dve.wait_ge(gate_step, 7 + 2 * (R - 1))
            dve.scalar_tensor_tensor(out=gates[:, S:E, :].rearrange("p e t -> p t e"), in0=rank[:, :, :], scalar=float(TOP),
                                     in1=prob[:, :, :], op0=ALU.is_lt, op1=ALU.mult).then_inc(gates_done, 1)
            for k in range(NC):
                dve.wait_ge(down_done, k + 1)
                dve.tensor_tensor(free(acc[:, TPC * k:TPC * k + TPC, :]), down[:, k % 2, :],
                                  free(s.normed[:, TPC * k:TPC * k + TPC, :]), ALU.add).then_inc(acc_done, 1)
                if k == NC - 2:
                    for g in range(NC - 1):
                        add_bias(g)
            add_bias(NC - 1)
            dve.wait_ge(bias_added, NC)
            with dve.Fori(0, (E - 1) // 2) as i:
                for c in range(2 * NC):
                    k = c % NC
                    n = i * 8 + (NC + c)
                    dve.wait_ge(down_done, n + 1)
                    dve.wait_ge(acc_done, n - 3)
                    for j in range(TPC):
                        t = TPC * k + j
                        add = dve.scalar_tensor_tensor(out=acc[:, t, :], in0=down[:, k % 2, P * j:P * j + P],
                                                       scalar=gates[:, bass.ds(i * 2 + (1 + c // NC), 1), t],
                                                       in1=acc[:, t, :], op0=ALU.mult, op1=ALU.add)
                    add.then_inc(acc_done, 1)
            for k in range(NC):
                dve.wait_ge(acc_done, (E - 1) * NC + k + 1)
                xk = free(s.x[:, TPC * k:TPC * k + TPC, :])
                dve.scalar_tensor_tensor(out=xk, in0=free(acc[:, TPC * k:TPC * k + TPC, :]), scalar=0.5, in1=xk,
                                         op0=ALU.mult, op1=ALU.add)

def layout_more(np, i):
    w1 = np.concatenate([i["L1_ffn_sW1"][:, :, :256], i["L1_ffn_sW1"][:, :, 256:], i["L1_ffn_rW1"]])
    b1 = np.concatenate([i["L1_ffn_sb1"].reshape(2, 256), i["L1_ffn_rb1"]])
    w2 = np.concatenate([i["L1_ffn_sW2"].reshape(2, 256, 128), i["L1_ffn_rW2"]])
    experts = np.concatenate([b1.reshape(17, 2, 128).transpose(0, 2, 1), w1,
                              w2.reshape(17, 2, 128, 128).transpose(0, 2, 1, 3).reshape(17, 128, 256)], axis=2)
    b2 = np.zeros((128, 128), np.float32)
    b2[0] = i["L1_ffn_sb2"][0]
    b2[2:17] = i["L1_ffn_rb2"]
    inv_freq = (1.0 / np.float32(6000.0) ** (np.arange(0, 32, 2, dtype=np.float32) / np.float32(32))).astype(np.float32)
    angle = np.outer(np.arange(1024, dtype=np.float32), inv_freq).astype(np.float32)
    cos, sin = np.cos(angle).T, np.sin(angle).T
    one, none = np.ones((32, 1024), np.float32), np.zeros((32, 1024), np.float32)
    c = np.concatenate([cos, cos, one] * 2)
    sn = np.concatenate([-sin, sin, none] * 2)
    rope = np.stack([c / 8, sn / 8, c, sn], axis=1).astype(np.float32)
    wq, wk, wv = i["L1_attn_W_qkv"]
    attn_in = np.zeros((9, 128, 3, 128), np.float32)
    for n, w in enumerate((wq, wk, wv)):
        attn_in[:8, :, n] = w.reshape(8, 128, 128).transpose(0, 2, 1)
    attn_out = i["L1_attn_W_o"].reshape(128, 8, 128).transpose(1, 2, 0)
    causal = np.triu(np.full((128, 128), -1e30, np.float32), 1)
    vec = lambda name: i["L0_attn_" + name].reshape(128)
    maa = np.stack([vec("time_maa_" + f) for f in "wkvrgx"] + [vec("time_decay"), vec("ln_w"), vec("ln_b")], axis=1)
    maa_w1 = np.zeros((128, 256), np.float32)
    maa_w1[:, :160] = i["L0_attn_time_maa_w1"]
    maa_w2 = np.zeros((128, 5, 128), np.float32)
    for f in range(5):
        maa_w2[32 * (f % 4):32 * (f % 4) + 32, f] = i["L0_attn_time_maa_w2"][f]
    decay_w1, decay_w2 = np.zeros((128, 128), np.float32), np.zeros((128, 128), np.float32)
    decay_w1[:, :64], decay_w2[:64] = i["L0_attn_time_decay_w1"], i["L0_attn_time_decay_w2"]
    mix_w = np.stack([decay_w1] + [i["L0_attn_W_" + f].T for f in "kvrg"], axis=1)
    head = np.arange(128) // 8
    return {
        "maa": maa,
        "maa_w1": maa_w1.reshape(128, 2, 128),
        "maa_w2": maa_w2,
        "mix_w": mix_w,
        "decay_w2": decay_w2,
        "decay_w_out": i["L0_attn_W_o"].T,
        "same_head": (head[:, None] == head[None, :]).astype(np.float32),
        "head_of": (head[:, None] == np.arange(16)[None, :]).astype(np.float32),
        "key_later": np.tril(np.ones((128, 128), np.float32), -1),
        "rope": rope,
        "attn_in": attn_in.reshape(9, 128, 384),
        "attn_out": attn_out,
        "causal": causal,
        "experts": experts,
        "expert_b2": b2,
        "gate_w": i["L1_ffn_gW"],
        "gate_b": np.broadcast_to(i["L1_ffn_gb"], (128, 15)),
    }


STAGES = 6


def program(nc, d, out):
    with ExitStack() as ctx:
        def sb(name, shape, dt=F32):
            return ctx.enter_context(nc.sbuf_tensor(name, shape, dt))

        s = Store()
        s.semaphores = ctx
        s.x = sb("x", [P, NT, D])
        s.xT = sb("xT", [P, B, T + 2])
        s.normed = sb("normed", [P, NT, D])
        s.gate_w = sb("gate_w", [P, 15])
        s.gate_b = sb("gate_b", [P, 15])
        s.expert_b2 = sb("expert_b2", [P, D])
        s.rope = sb("rope", [P, 4, T])
        s.causal_f = sb("causal_f", [P, P])
        s.causal = sb("causal", [P, P], BF16)
        s.ident_bf = sb("ident_bf", [P, P], BF16)
        s.tables_loaded = ctx.enter_context(nc.semaphore("tables_loaded"))
        s.maa = sb("maa", [P, 9])
        s.maa_w1 = sb("maa_w1", [P, 2, P])
        s.maa_w2 = sb("maa_w2", [P, 5, P])
        s.mix_w = sb("mix_w", [P, 5, P])
        s.decay_w2 = sb("decay_w2", [P, P])
        s.decay_w_out = sb("decay_w_out", [P, P])
        s.same_head = sb("same_head", [P, P])
        s.head_of = sb("head_of", [P, 16])
        s.key_later_f = sb("key_later_f", [P, P])
        s.key_later = sb("key_later", [P, P], mybir.dt.uint8)
        s.ident = sb("ident", [P, P])
        s.w_fc = sb("w_fc", [P, 512])
        s.w_proj = sb("w_proj", [P, 4, D])
        s.ffn_ln = sb("ffn_ln", [P, 2, 4])
        load_phase(nc, s, d)
        ternary_phase(nc, s)
        steps = [lambda g: ternary_ffn_phase(nc, s, g), lambda g: decay_attention_phase(nc, s, d, g),
                 lambda g: ternary_ffn_phase(nc, s, g), lambda g: expert_ffn_phase(nc, s, d, g),
                 lambda g: softmax_attention_phase(nc, s, d, g), lambda g: expert_ffn_phase(nc, s, d, g)]
        for n, step in enumerate(steps[:STAGES]):
            layernorm_phase(nc, s, f"norm{n}")
            step(f"layer{n}")
        store_phase(nc, s, out)


def kernel(**inputs):
    import numpy as _np
    import concourse.bacc as _bacc
    from concourse import mybir as _mybir
    from concourse.bass_utils import run_bass_kernel_spmd as _run

    i = {k: _np.asarray(v) for k, v in inputs.items()}
    lay = {
        "x": i["L0_attn_x"],
        "eye": _np.eye(128, dtype=_np.float32),
        "w_fc": i["L0_ffn_W_fc"].T,
        "w_proj": i["L0_ffn_W_proj"].T,
        "ffn_ln": _np.stack([i["L0_ffn_ln_w"].reshape(4, 128).T, i["L0_ffn_ln_b"].reshape(4, 128).T], axis=1),
    }
    lay.update(layout_more(_np, i))
    nc = _bacc.Bacc("TRN2", target_bir_lowering=False, num_devices=1)
    arrays, d = {}, {}
    for name, a in lay.items():
        a = _np.ascontiguousarray(a)
        arrays[f"in_{name}"] = a
        d[name] = nc.dram_tensor(f"in_{name}", a.shape, _mybir.dt.from_np(a.dtype), kind="ExternalInput").ap()
    out = nc.dram_tensor("out_0", (2, 1024, 128), _mybir.dt.float32, kind="ExternalOutput").ap()
    program(nc, d, out)
    r = _run(nc, [arrays], core_ids=[0])
    return r.results[0]["out_0"]
```

```python
from contextlib import ExitStack

import concourse.bass as bass
from concourse import mybir

ALU = mybir.AluOpType
ACT = mybir.ActivationFunctionType
F32 = mybir.dt.float32
F32R = mybir.dt.float32r
BF16 = mybir.dt.bfloat16
U8 = mybir.dt.uint8
AX_X = mybir.AxisListType.X

P = 128
D = 128
B = 2
T = 1024
NT = B * T // P
NC = B * T // 512
TPC = 512 // P
LN_EPS = 1e-5


class Store:
    pass


def free(ap):
    return ap.rearrange("p a b -> p (a b)")


def token_tile(xT, t):
    per = T // P
    return xT[:, t // per, 1 + P * (t % per):1 + P * (t % per + 1)]


def token_chunk(xT, k):
    per = T // 512
    return xT[:, k // per, 1 + 512 * (k % per):1 + 512 * (k % per + 1)]


def layernorm_phase(nc, s, tag):
    with ExitStack() as ctx:
        def sem(name):
            return s.semaphores.enter_context(nc.semaphore(f"{tag}_{name}"))

        stats = ctx.enter_context(nc.sbuf_tensor(f"{tag}_stats", [P, NT, 6], F32))
        moments = ctx.enter_context(nc.sbuf_tensor(f"{tag}_moments", [P, NT, 2], F32))
        var_eps = ctx.enter_context(nc.sbuf_tensor(f"{tag}_var_eps", [P, NT], F32))
        std = ctx.enter_context(nc.sbuf_tensor(f"{tag}_std", [P, NT], F32))
        rstd = ctx.enter_context(nc.sbuf_tensor(f"{tag}_rstd", [P, NT], F32))
        spare = ctx.enter_context(nc.sbuf_tensor(f"{tag}_spare", [P, 1], F32))
        turned = ctx.enter_context(nc.psum_tensor(f"{tag}_turned", [P, 4, 512], F32))
        stats_step = sem("stats_step")
        std_done, normed_done = sem("std_done"), sem("normed_done")
        turned_done = sem("turned_done")
        block = ctx.enter_context(nc.Block())

        @block.vector
        def _(dve):
            for t in range(NT):
                dve.bn_stats(stats[:, t, :], s.x[:, t, :]).then_inc(stats_step, 1)
            for t in range(NT):
                dve.wait_ge(stats_step, t + 1)
                dve.bn_aggr(moments[:, t, :], stats[:, t, :]).then_inc(stats_step, 1)
            dve.wait_ge(stats_step, 2 * NT)
            dve.tensor_scalar(var_eps[:, :], moments[:, :, 1], LN_EPS, None, ALU.add).then_inc(stats_step, 1)
            dve.wait_ge(std_done, 1)
            dve.reciprocal(rstd[:, :], std[:, :]).then_inc(stats_step, 1)
            dve.wait_ge(stats_step, 2 * NT + 2)
            for t in range(NT):
                dve.tensor_scalar(s.normed[:, t, :], s.x[:, t, :], moments[:, t, 0:1], rstd[:, t:t + 1],
                                  ALU.subtract, ALU.mult).then_inc(normed_done, 1)

        @block.scalar
        def _(act):
            act.activation(spare[:, :], s.ident[:, 0:1], ACT.Sqrt)
            act.wait_ge(stats_step, 2 * NT + 1)
            act.activation(std[:, :], var_eps[:, :], ACT.Sqrt).then_inc(std_done, 1)
            for k in range(NC):
                act.wait_ge(turned_done, k + 1)
                act.activation(token_chunk(s.xT, k), turned[:, k, :], ACT.Copy)

        @block.tensor
        def _(pe):
            for t in range(NT):
                pe.wait_ge(normed_done, t + 1)
                turn = pe.transpose(turned[:, t // TPC, P * (t % TPC):P * (t % TPC + 1)], s.normed[:, t, :], s.ident[:, :])
                if t % TPC == TPC - 1:
                    turn.then_inc(turned_done, 1)


def load_phase(nc, s, d):
    with ExitStack() as ctx:
        loaded = ctx.enter_context(nc.semaphore("loaded"))
        block = ctx.enter_context(nc.Block())

        @block.sync
        def _(sp):
            sp.dma_start(s.x[:, :, :], d["x"].rearrange("b (n p) c -> p (b n) c", p=P)).then_inc(loaded, 16)
            sp.dma_start(s.ident[:, :], d["eye"]).then_inc(loaded, 16)
            sp.dma_start(s.w_fc[:, :], d["w_fc"]).then_inc(loaded, 16)
            sp.dma_start(s.w_proj[:, :, :], d["w_proj"].rearrange("(n p) c -> p n c", p=P)).then_inc(loaded, 16)
            sp.dma_start(s.ffn_ln[:, :, :], d["ffn_ln"]).then_inc(loaded, 16)
            sp.dma_start(s.gate_w[:, :], d["gate_w"]).then_inc(s.other_loaded, 16)
            sp.dma_start(s.gate_b[:, :], d["gate_b"]).then_inc(s.other_loaded, 16)
            sp.dma_start(s.expert_b2[:, :], d["expert_b2"]).then_inc(s.other_loaded, 16)
            sp.dma_start(s.causal_f[:, :], d["causal"]).then_inc(s.other_loaded, 16)
            sp.dma_start(s.rope[:, :, :], d["rope"]).then_inc(s.tables_loaded, 16)
            for to, name in ((s.maa[:, :], "maa"), (s.maa_w1[:, :, :], "maa_w1"), (s.maa_w2[:, :, :], "maa_w2"),
                             (s.mix_w[:, :, :], "mix_w"), (s.decay_w2[:, :], "decay_w2"),
                             (s.decay_w_out[:, :], "decay_w_out"), (s.same_head[:, :], "same_head"), (s.head_mean[:, :], "head_mean"),
                             (s.head_of[:, :], "head_of"), (s.rest_holds_f[:, :], "rest_holds")):
                sp.dma_start(to, d[name]).then_inc(s.other_loaded, 16)
            sp.wait_ge(loaded, 16 * 5)

        @block.vector
        def _(dve):
            dve.memset(s.xT[:, :, :], 0.0)


def masks_phase(nc, s):
    with ExitStack() as ctx:
        block = ctx.enter_context(nc.Block())

        @block.vector
        def _(dve):
            dve.wait_ge(s.other_loaded, 16 * 14)
            dve.tensor_copy(s.causal[:, :], s.causal_f[:, :])
            dve.tensor_copy(s.rest_holds[:, :], s.rest_holds_f[:, :])
            dve.tensor_copy(s.ident_bf[:, :], s.ident[:, :])


def ternary_phase(nc, s):
    with ExitStack() as ctx:
        def sem(name):
            return s.semaphores.enter_context(nc.semaphore(f"tern_{name}"))

        ones = ctx.enter_context(nc.sbuf_tensor("tern_ones", [P, P], F32))
        part = ctx.enter_context(nc.sbuf_tensor("tern_part", [P, 2], F32))
        bound = ctx.enter_context(nc.sbuf_tensor("tern_bound", [P, 4], F32))
        above = ctx.enter_context(nc.sbuf_tensor("tern_above", [P, 2, 512], F32))
        below = ctx.enter_context(nc.sbuf_tensor("tern_below", [P, 2, 512], F32))
        total = ctx.enter_context(nc.psum_tensor("tern_total", [P, 2], F32))
        ones_done, part_done, total_done = sem("ones_done"), sem("part_done"), sem("total_done")
        bound_done, compared = sem("bound_done"), sem("compared")
        block = ctx.enter_context(nc.Block())
        weights = (s.w_fc[:, :], free(s.w_proj[:, :, :]))
        count = float(4 * D * D)

        @block.gpsimd
        def _(pool):
            pool.memset(ones[:, :], 1.0).then_inc(ones_done, 1)

        @block.vector
        def _(dve):
            for n, w in enumerate(weights):
                dve.tensor_reduce(part[:, n:n + 1], w, AX_X, ALU.add, apply_absolute_value=True).then_inc(part_done, 1)
            dve.wait_ge(total_done, 1)
            dve.tensor_scalar(bound[:, 0:2], total[:, :], 1.0 / count, 1e-6, ALU.mult, ALU.add).then_inc(bound_done, 1)
            dve.wait_ge(bound_done, 1)
            dve.tensor_scalar(bound[:, 2:4], bound[:, 0:2], -0.5, None, ALU.mult).then_inc(bound_done, 1)
            dve.wait_ge(bound_done, 2)
            dve.tensor_scalar(bound[:, 0:2], bound[:, 0:2], 0.5, None, ALU.mult).then_inc(bound_done, 1)
            dve.wait_ge(bound_done, 3)
            for n, w in enumerate(weights):
                dve.tensor_scalar(above[:, n, :], w, bound[:, n:n + 1], None, ALU.is_gt).then_inc(compared, 1)
                dve.tensor_scalar(below[:, n, :], w, bound[:, n + 2:n + 3], None, ALU.is_lt).then_inc(compared, 1)
            dve.wait_ge(compared, 4)
            for n, w in enumerate(weights):
                dve.tensor_tensor(w, above[:, n, :], below[:, n, :], ALU.subtract)

        @block.tensor
        def _(pe):
            pe.wait_ge(ones_done, 1)
            pe.wait_ge(part_done, 2)
            pe.matmul(total[:, :], ones[:, :], part[:, :], start=True, stop=True).then_inc(total_done, 1)


def ternary_ffn_phase(nc, s, tag):
    HB = 4
    with ExitStack() as ctx:
        def sem(name):
            return s.semaphores.enter_context(nc.semaphore(f"{tag}_{name}"))

        def sb(name, shape):
            return ctx.enter_context(nc.sbuf_tensor(f"{tag}_{name}", shape, F32))

        def ps(name, shape):
            return ctx.enter_context(nc.psum_tensor(f"{tag}_{name}", shape, F32))

        hidden = sb("hidden", [P, NT, 512])
        hiddenT = sb("hiddenT", [P, HB, NT * P])
        stats, moments = sb("stats", [P, NT, 6]), sb("moments", [P, NT, 2])
        var_eps, std, rstd = sb("var_eps", [P, NT]), sb("std", [P, NT]), sb("rstd", [P, NT])
        up = ps("up", [P, 2, 512])
        turned = ps("turned", [P, 4, 512])
        down = ps("down", [P, 2, 512])
        up_done, gelu_done, stats_step = sem("up_done"), sem("gelu_done"), sem("stats_step")
        std_done = sem("std_done")
        normed_done, turned_done, even_copied, odd_copied = sem("normed_done"), sem("turned_done"), sem("even_copied"), sem("odd_copied")
        down_done, added = sem("down_done"), sem("added")
        block = ctx.enter_context(nc.Block())

        @block.tensor
        def _(pe):
            for t in range(NT):
                if t >= 2:
                    pe.wait_ge(gelu_done, t - 1)
                pe.matmul(up[:, t % 2, :], token_tile(s.xT, t), s.w_fc[:, :], start=True, stop=True).then_inc(up_done, 1)

            def turn_chunk(k):
                pe.wait_ge(normed_done, TPC * (k + 1))
                for hb in range(HB):
                    if k >= 1:
                        copied = even_copied if hb % 2 == 0 else odd_copied
                        pe.wait_ge(copied, 2 * (k - 1) + hb // 2 + 1)
                    for j in range(TPC):
                        turn = pe.transpose(turned[:, hb, P * j:P * j + P],
                                            hidden[:, TPC * k + j, P * hb:P * hb + P], s.ident[:, :])
                    turn.then_inc(turned_done, 1)

            def down_chunk(k):
                pe.wait_ge(even_copied, 2 * (k + 1))
                pe.wait_ge(odd_copied, 2 * (k + 1))
                if k >= 2:
                    pe.wait_ge(added, k - 1)
                for j in range(TPC):
                    for hb in range(HB):
                        at = 512 * k + P * j
                        mm = pe.matmul(down[:, k % 2, P * j:P * j + P], hiddenT[:, hb, at:at + P], s.w_proj[:, hb, :],
                                       start=(hb == 0), stop=(hb == HB - 1))
                mm.then_inc(down_done, 1)

            turn_chunk(0)
            for k in range(NC):
                if k + 1 < NC:
                    turn_chunk(k + 1)
                down_chunk(k)

        @block.scalar
        def _(act):
            for t in range(NT):
                act.wait_ge(up_done, t + 1)
                act.activation(hidden[:, t, :], up[:, t % 2, :], ACT.Gelu).then_inc(gelu_done, 1)
            act.wait_ge(stats_step, 2 * NT + 1)
            act.activation(std[:, :], var_eps[:, :], ACT.Sqrt).then_inc(std_done, 1)
            for k in range(NC):
                for hb in (0, 2):
                    act.wait_ge(turned_done, HB * k + hb + 1)
                    act.activation(hiddenT[:, hb, 512 * k:512 * k + 512], turned[:, hb, :], ACT.Identity,
                                   scale=s.ffn_ln[:, 0, hb:hb + 1], bias=s.ffn_ln[:, 1, hb:hb + 1]).then_inc(even_copied, 1)

        @block.vector
        def _(dve):
            for t in range(NT):
                dve.wait_ge(gelu_done, t + 1)
                dve.bn_stats(stats[:, t, :], hidden[:, t, :]).then_inc(stats_step, 1)
            for t in range(NT):
                dve.wait_ge(stats_step, t + 1)
                dve.bn_aggr(moments[:, t, :], stats[:, t, :]).then_inc(stats_step, 1)
            dve.wait_ge(stats_step, 2 * NT)
            dve.tensor_scalar(var_eps[:, :], moments[:, :, 1], LN_EPS, None, ALU.add).then_inc(stats_step, 1)
            dve.wait_ge(std_done, 1)
            dve.reciprocal(rstd[:, :], std[:, :]).then_inc(stats_step, 1)
            dve.wait_ge(stats_step, 2 * NT + 2)

            def norm_chunk(k):
                for t in range(TPC * k, TPC * k + TPC):
                    dve.tensor_scalar(hidden[:, t, :], hidden[:, t, :], moments[:, t, 0:1], rstd[:, t:t + 1],
                                      ALU.subtract, ALU.mult).then_inc(normed_done, 1)

            norm_chunk(0)
            for k in range(NC):
                if k + 1 < NC:
                    norm_chunk(k + 1)
                for hb in (1, 3):
                    dve.wait_ge(turned_done, HB * k + hb + 1)
                    dve.tensor_scalar(hiddenT[:, hb, 512 * k:512 * k + 512], turned[:, hb, :],
                                      s.ffn_ln[:, 0, hb:hb + 1], s.ffn_ln[:, 1, hb:hb + 1],
                                      ALU.mult, ALU.add).then_inc(odd_copied, 1)
                dve.wait_ge(down_done, k + 1)
                xk = free(s.x[:, TPC * k:TPC * k + TPC, :])
                dve.scalar_tensor_tensor(out=xk, in0=down[:, k % 2, :], scalar=0.5, in1=xk,
                                         op0=ALU.mult, op1=ALU.add).then_inc(added, 1)


def store_phase(nc, s, out):
    with ExitStack() as ctx:
        stored = ctx.enter_context(nc.semaphore("stored"))
        block = ctx.enter_context(nc.Block())

        @block.sync
        def _(sp):
            sp.dma_start(out.rearrange("b (n p) c -> p (b n) c", p=P), s.x[:, :, :]).then_inc(stored, 16)
            sp.wait_ge(stored, 16)


def mix_phase(nc, s, a, tag):
    with ExitStack() as ctx:
        def sem(name):
            return s.semaphores.enter_context(nc.semaphore(f"{tag}_{name}"))

        def sb(name, shape, dt=F32):
            return ctx.enter_context(nc.sbuf_tensor(f"{tag}_{name}", shape, dt))

        def ps(name, shape):
            return ctx.enter_context(nc.psum_tensor(f"{tag}_{name}", shape, F32))

        F = 5
        N = F * NC
        dx, xx = sb("dx", [P, B, T]), sb("xx", [P, B, T])
        low = sb("low", [P, 2, B * T])
        part = sb("part", [P, 2, 512])
        mixed = sb("mixed", [P, 3, 512])
        decay_low = sb("decay_low", [P, B * T])
        mm_bank, proj_bank, decay_bank = ps("mm", [P, 2, 512]), ps("proj", [P, 2, 512]), ps("decay", [P, 2, 512])
        shift_step, low_done, low_copied = sem("shift_step"), sem("low_done"), sem("low_copied")
        mm_done, part_done, mixed_done, proj_done, proj_copied = (sem("mm_done"), sem("part_done"), sem("mixed_done"),
                                                                  sem("proj_done"), sem("proj_copied"))
        decay_done, decay_copied = sem("decay_done"), sem("decay_copied")
        block = ctx.enter_context(nc.Block())

        def flat(ap, k):
            return ap[:, 512 * k:512 * k + 512]

        def chunk(ap, k):
            return ap[:, k // 2, 512 * (k % 2):512 * (k % 2) + 512]

        @block.vector
        def _(dve):
            middle = s.xT[:, :, 1:T + 1]
            dve.tensor_tensor(xx[:, :, :], s.xT[:, :, 0:T], s.xT[:, :, 2:T + 2], ALU.add).then_inc(shift_step, 1)
            dve.wait_ge(shift_step, 1)
            dve.scalar_tensor_tensor(out=dx[:, :, :], in0=xx[:, :, :], scalar=0.5, in1=middle,
                                     op0=ALU.mult, op1=ALU.subtract).then_inc(shift_step, 1)
            dve.wait_ge(shift_step, 2)
            dve.scalar_tensor_tensor(out=xx[:, :, :], in0=dx[:, :, :], scalar=s.maa[:, F:F + 1], in1=middle,
                                     op0=ALU.mult, op1=ALU.add).then_inc(shift_step, 1)
            for n in range(N):
                f, k = n // NC, n % NC
                dve.wait_ge(mm_done, n + 1)
                if n >= 2:
                    dve.wait_ge(mixed_done, n - 1)
                dve.scalar_tensor_tensor(out=part[:, n % 2, :], in0=mm_bank[:, n % 2, :], scalar=s.maa[:, f:f + 1],
                                         in1=chunk(dx, k), op0=ALU.add, op1=ALU.mult).then_inc(part_done, 1)

        @block.gpsimd
        def _(pool):
            for n in range(N):
                pool.wait_ge(part_done, n + 1)
                if n >= 3:
                    pool.wait_ge(proj_done, n - 2)
                pool.tensor_tensor(mixed[:, n % 3, :], part[:, n % 2, :], token_chunk(s.xT, n % NC), ALU.add)\
                    .then_inc(mixed_done, 1)

        @block.tensor
        def _(pe):
            pe.wait_ge(shift_step, 3)
            for n in range(2 * NC):
                k, half = n // 2, n % 2
                if n >= 2:
                    pe.wait_ge(low_copied, n - 1)
                pe.matmul(proj_bank[:, half, :], s.maa_w1[:, half, :], chunk(xx, k), start=True, stop=True)\
                  .then_inc(low_done, 1)

            def project(n):
                f = n // NC
                pe.wait_ge(mixed_done, n + 1)
                if n < 2:
                    pe.wait_ge(low_copied, 2 * NC - 1 + n)
                else:
                    pe.wait_ge(proj_copied, n - 1)
                if f == 2:
                    for j in range(TPC):
                        mm = pe.matmul(proj_bank[:, n % 2, P * j:P * j + P], mixed[:, n % 3, P * j:P * j + P],
                                       s.mix_w[:, f, :], start=True, stop=True)
                else:
                    mm = pe.matmul(proj_bank[:, n % 2, :], s.mix_w[:, f, :], mixed[:, n % 3, :], start=True, stop=True)
                mm.then_inc(proj_done, 1)

            for n in range(N + 2):
                if n < N:
                    f, k = n // NC, n % NC
                    if n < NC:
                        pe.wait_ge(low_copied, 2 * (k + 1))
                    if n >= 2:
                        pe.wait_ge(part_done, n - 1)
                    pe.matmul(mm_bank[:, n % 2, :], s.maa_w2[:, f, :], flat(low[:, f // 4, :], k), start=True, stop=True)\
                      .then_inc(mm_done, 1)
                if n >= 2:
                    project(n - 2)
                if n >= 8 and n - 8 < NC:
                    k = n - 8
                    pe.wait_ge(proj_copied, k + 1)
                    if k >= 2:
                        pe.wait_ge(decay_copied, k - 1)
                    pe.matmul(decay_bank[:, k % 2, :], s.decay_w2[:, :], flat(decay_low, k), start=True, stop=True)\
                      .then_inc(decay_done, 1)

        @block.scalar
        def _(act):
            for n in range(2 * NC):
                act.wait_ge(low_done, n + 1)
                act.activation(flat(low[:, n % 2, :], n // 2), proj_bank[:, n % 2, :], ACT.Tanh).then_inc(low_copied, 1)
            for n in range(N):
                f, k = n // NC, n % NC
                act.wait_ge(proj_done, n + 1)
                to, func = ((flat(decay_low, k), ACT.Tanh), (flat(a.k, k), ACT.Copy), (flat(free(a.v[:, :, :]), k), ACT.Copy),
                            (flat(a.r, k), ACT.Copy), (flat(a.g, k), ACT.Silu))[f]
                act.activation(to, proj_bank[:, n % 2, :], func).then_inc(proj_copied, 1)
                if NC + 2 <= n < 2 * NC + 2:
                    k = n - NC - 2
                    act.wait_ge(decay_done, k + 1)
                    act.activation(flat(a.rate, k), decay_bank[:, k % 2, :], ACT.Exp, bias=s.maa[:, 6:7])\
                       .then_inc(decay_copied, 1)


def decay_phase(nc, s, a, tag):
    with ExitStack() as ctx:
        def sem(name):
            return s.semaphores.enter_context(nc.semaphore(f"{tag}_{name}"))

        zeros = ctx.enter_context(nc.sbuf_tensor(f"{tag}_zeros", [P, T], F32))
        run = ctx.enter_context(nc.sbuf_tensor(f"{tag}_run", [P, 2, B, T], F32))
        clip = ctx.enter_context(nc.sbuf_tensor(f"{tag}_clip", [P, 2, B, T], F32))
        zeroed, run_step, lowered, clipped, grown = sem("zeroed"), sem("run_step"), sem("lowered"), sem("clipped"), sem("grown")
        block = ctx.enter_context(nc.Block())
        MID = T // 2
        FWD, BWD = 0, 1
        FACTORS = ((a.qf, FWD, 1.0, a.r), (a.kf, FWD, -1.0, a.k), (a.qb, BWD, -1.0, a.r), (a.kb, BWD, 1.0, a.k))

        BY_POOL = (1, 3)

        def of(ap, b):
            return ap[:, T * b:T * b + T]

        @block.gpsimd
        def _(pool):
            pool.memset(zeros[:, :], 0.0).then_inc(zeroed, 1)
            for b in range(B):
                for n, (out, way, sign, operand) in enumerate(FACTORS):
                    if n in BY_POOL:
                        pool.wait_ge(grown, 4 * b + n + 1)
                        pool.tensor_tensor(of(out, b), of(out, b), of(operand, b), ALU.mult)

        @block.vector
        def _(dve):
            dve.wait_ge(zeroed, 1)
            for b in range(B):
                dve.tensor_tensor_scan(run[:, FWD, b, :], zeros[:, :], of(a.rate, b), 0.0, ALU.add, ALU.subtract)\
                   .then_inc(run_step, 1)
                dve.wait_ge(run_step, 2 * b + 1)
                dve.tensor_tensor(run[:, BWD, b, :], run[:, FWD, b, :], of(a.rate, b), ALU.add).then_inc(run_step, 1)
                dve.wait_ge(run_step, 2 * b + 2)
                for way in (FWD, BWD):
                    dve.tensor_scalar(clip[:, way, b, :], run[:, way, b, :], run[:, way, b, MID:MID + 1], -60.0,
                                      ALU.subtract, ALU.max).then_inc(lowered, 1)
                for way in (FWD, BWD):
                    dve.wait_ge(lowered, 2 * b + way + 1)
                    dve.tensor_scalar(clip[:, way, b, :], clip[:, way, b, :], 60.0, None, ALU.min).then_inc(clipped, 1)
            for b in range(B):
                for n, (out, way, sign, operand) in enumerate(FACTORS):
                    if n not in BY_POOL:
                        dve.wait_ge(grown, 4 * b + n + 1)
                        dve.tensor_tensor(of(out, b), of(out, b), of(operand, b), ALU.mult)

        @block.scalar
        def _(act):
            for b in range(B):
                for n, (out, way, sign, operand) in enumerate(FACTORS):
                    act.wait_ge(clipped, 2 * b + way + 1)
                    act.activation(of(out, b), clip[:, way, b, :], ACT.Exp, scale=sign).then_inc(grown, 1)


def state_phase(nc, s, a, tag):
    TB = T // P
    with ExitStack() as ctx:
        def sem(name):
            return s.semaphores.enter_context(nc.semaphore(f"{tag}_{name}"))

        tokens = ctx.enter_context(nc.sbuf_tensor(f"{tag}_tokens", [P, 2, NT, P], F32))
        turned = ctx.enter_context(nc.psum_tensor(f"{tag}_turned", [P, 2, 512], F32))
        outer = ctx.enter_context(nc.psum_tensor(f"{tag}_outer", [P, 4, 512], F32))
        own = ctx.enter_context(nc.sbuf_tensor(f"{tag}_own", [P, 2, NT, P], F32))
        turned_done, tokens_done, outer_done, own_done, summed = (sem("turned_done"), sem("tokens_done"), sem("outer_done"),
                                                                  sem("own_done"), (sem("fwd_summed"), sem("bwd_summed")))
        block = ctx.enter_context(nc.Block())
        GROUPS = [(way, k) for k in range(NC) for way in (1, 0)]

        def running_sums(eng, way):
            eng.wait_ge(own_done, len(GROUPS))
            for n in range(1, TB):
                c = n if way == 0 else TB - 1 - n
                last = c - 1 if way == 0 else c + 1
                to, mine, held = a.state[:, way, c::TB, :], own[:, way, last::TB, :], a.state[:, way, last::TB, :]
                if n == 1:
                    eng.tensor_copy(to, mine).then_inc(summed[way], 1)
                else:
                    eng.wait_ge(summed[way], n - 1)
                    eng.tensor_tensor(to, mine, held, ALU.add).then_inc(summed[way], 1)

        @block.tensor
        def _(pe):
            for n in range(len(GROUPS) + 1):
                if n < len(GROUPS):
                    way, k = GROUPS[n]
                    keys = a.kf if way == 0 else a.kb
                    if n >= 2:
                        pe.wait_ge(tokens_done, n - 1)
                    for j in range(TPC):
                        at = 512 * k + P * j
                        mm = pe.transpose(turned[:, n % 2, P * j:P * j + P], keys[:, at:at + P], s.ident[:, :])
                    mm.then_inc(turned_done, 1)
                if n >= 1:
                    way, k = GROUPS[n - 1]
                    pe.wait_ge(tokens_done, n)
                    if n - 1 >= 4:
                        pe.wait_ge(own_done, n - 4)
                    for j in range(TPC):
                        t = TPC * k + j
                        mm = pe.matmul(outer[:, (n - 1) % 4, P * j:P * j + P], tokens[:, way, t, :], a.v[:, t, :],
                                       start=True, stop=True)
                    mm.then_inc(outer_done, 1)

        @block.scalar
        def _(act):
            for n, (way, k) in enumerate(GROUPS):
                act.wait_ge(turned_done, n + 1)
                act.activation(free(tokens[:, way, TPC * k:TPC * k + TPC, :]), turned[:, n % 2, :], ACT.Copy)\
                   .then_inc(tokens_done, 1)

        @block.vector
        def _(dve):
            same_head = s.same_head[:, :].unsqueeze(1).to_broadcast([P, TPC, P])
            for n, (way, k) in enumerate(GROUPS):
                dve.wait_ge(outer_done, n + 1)
                dve.tensor_tensor(own[:, way, TPC * k:TPC * k + TPC, :],
                                  outer[:, n % 4, :].rearrange("p (t c) -> p t c", t=TPC), same_head, ALU.mult)\
                   .then_inc(own_done, 1)
            running_sums(dve, 1)

        @block.gpsimd
        def _(pool):
            running_sums(pool, 0)


def chunk_phase(nc, s, a, tag):
    H, K, HQ = 16, 8, 4
    TB = T // P
    G = H // HQ
    N = NT * G
    EPS = 1e-05 * 64.0
    DIAGONAL = P + K
    COPY, MEAN, CENTER, SQUARE, VAR, STD, INVERT, GATE, MIX, ADD = 18, 20, 20, 20, 22, 22, 23, 27, 29, 30
    RING = 3
    HALF = P // 2
    AHEAD = 3
    END = N - TPC * G + ADD + 1
    with ExitStack() as ctx:
        def sem(name):
            return s.semaphores.enter_context(nc.semaphore(f"{tag}_{name}"))

        def sb(name, shape):
            return ctx.enter_context(nc.sbuf_tensor(f"{tag}_{name}", shape, F32))

        def ps(name, shape):
            return ctx.enter_context(nc.psum_tensor(f"{tag}_{name}", shape, F32))

        per_head = sb("per_head", [P, 2, 2, H, P])
        v_per_head = sb("v_per_head", [P, 2, HQ * DIAGONAL])
        score = sb("score", [P, 4, HQ, P])
        y, eps = sb("y", [P, 2, 512]), sb("eps", [P, 1])
        square, std, rstd = sb("square", [P, 512]), sb("std", [P, 512]), sb("rstd", [P, 512])
        gated = sb("gated", [P, 2, 512])
        most, rest = ps("most", [P, RING, HQ, P]), ps("rest", [P, 2, 512])
        y_bank = ps("y_bank", [P, 2, 512])
        moment = mixed = ps("moment", [P, 512])
        fwd_spread, bwd_spread, scored, copied, merged, y_done, y_copied = (
            sem("fwd_spread"), sem("bwd_spread"), sem("scored"), sem("copied"), sem("merged"), sem("y_done"), sem("y_copied"))
        zeroed, v_spread, mean_done, centered = sem("zeroed"), sem("v_spread"), sem("mean_done"), sem("centered")
        squared, var_done, std_done, gate_step = sem("squared"), sem("var_done"), sem("std_done"), sem("gate_step")
        inverted = sem("inverted")
        mixed_done, added = sem("mixed_done"), sem("added")
        block = ctx.enter_context(nc.Block())

        def chunk_at(n, lag):
            steps = TPC * G
            return (n - lag) // steps if (n - lag) % steps == 0 and 0 <= n - lag < N else -1

        def spread(eng, n, way):
            t, heads = n // G, slice(HQ * (n % G), HQ * (n % G) + HQ)
            src = (a.qf if way == 0 else a.qb)[:, P * t:P * t + P]
            return eng.tensor_tensor(per_head[:, t % 2, way, heads, :], src.unsqueeze(1).to_broadcast([P, HQ, P]),
                                     s.head_of[:, heads].unsqueeze(2).to_broadcast([P, HQ, P]), ALU.mult)

        @block.gpsimd
        def _(pool):
            pool.memset(v_per_head[:, :, :], 0.0).then_inc(zeroed, 1)
            pool.memset(eps[:, :], EPS).then_inc(zeroed, 1)
            pool.wait_ge(zeroed, 2)
            for t in range(NT):
                if t >= 2:
                    pool.wait_ge(y_done, t - 1)
                heads = v_per_head[:, t % 2, :].rearrange("p (j x) -> p j x", x=DIAGONAL)[:, :, 0:P]
                pool.tensor_copy(heads.rearrange("p j (g y) -> p j g y", g=G)[:, :, :, 0:K],
                                 a.v[:, t, :].rearrange("p (g j k) -> p j g k", g=G, j=HQ)).then_inc(v_spread, 1)
                for n in range(G * t, G * t + G):
                    if t >= 2:
                        pool.wait_ge(scored, n - 2 * G + 1)
                    spread(pool, n, 1).then_inc(bwd_spread, 1)

        @block.tensor
        def _(pe):
            def scores(n):
                t, g = n // G, n % G
                pe.wait_ge(fwd_spread, n + 1)
                pe.wait_ge(bwd_spread, n + 1)
                if n >= RING:
                    pe.wait_ge(copied, n - RING + 1)
                if n >= 2:
                    pe.wait_ge(merged, n - 1)
                heads, lo, hi = slice(HQ * g, HQ * g + HQ), slice(0, HALF), slice(HALF, P)
                q_fwd, q_bwd = per_head[:, t % 2, 0, heads, :], per_head[:, t % 2, 1, heads, :]
                pe.matmul(most[:, n % RING, :, lo], a.kb[:, P * t:P * t + P], q_bwd[:, :, lo], start=True, stop=True,
                          skip_group_check=True)
                pe.matmul(most[:, n % RING, :, hi], a.kf[:, P * t:P * t + P], q_fwd[:, :, hi], start=True, stop=True,
                          skip_group_check=True)
                own = rest[:, n % 2, 0:HQ * HALF].rearrange("p (h i) -> p h i", h=HQ)
                pe.matmul(own[lo], a.kf[:, P * t:P * t + HALF], q_fwd[:, :, lo], start=True, stop=True)
                pe.matmul(own[hi], a.kb[:, P * t + HALF:P * t + P], q_bwd[:, :, hi], start=True, stop=True)\
                  .then_inc(scored, 1)

            def values(n):
                t, g = n // G, n % G
                c, to = t // TPC, slice(P * (t % TPC), P * (t % TPC) + P)
                at = slice(P * t, P * t + P)
                if g == 0:
                    if t % TPC == 0 and c >= 2:
                        pe.wait_ge(y_copied, c - 1)
                    pe.wait_ge(v_spread, t + 1)
                    first = True
                    for way, q in ((0, a.qf), (1, a.qb)):
                        if t % TB != (0 if way == 0 else TB - 1):
                            pe.matmul(y_bank[:, c % 2, to], a.state[:, way, t, :], q[:, at], start=first, stop=False,
                                      skip_group_check=True)
                            first = False
                pe.wait_ge(merged, n + 1)
                rows = P // G
                for j in range(HQ):
                    v_at = P * j + rows * g
                    mm = pe.matmul(y_bank[rows * g:rows * g + rows, c % 2, to], v_per_head[:, t % 2, v_at:v_at + rows],
                                   score[:, n % 4, j, :], start=False, stop=(j == HQ - 1), skip_group_check=True)
                if g == G - 1:
                    mm.then_inc(y_done, 1)

            for n in range(END):
                if n < N:
                    scores(n)
                if 2 <= n < N + 2:
                    values(n - 2)
                c = chunk_at(n, MEAN)
                if c >= 0:
                    pe.wait_ge(y_copied, c + 1)
                    if c >= 1:
                        pe.wait_ge(added, c)
                    pe.matmul(moment[:, :], s.head_mean[:, :], y[:, c % 2, :], start=True, stop=True).then_inc(mean_done, 1)
                c = chunk_at(n, VAR)
                if c >= 0:
                    pe.wait_ge(squared, c + 1)
                    pe.matmul(moment[:, :], s.head_mean[:, :], square[:, :], start=True, stop=True).then_inc(var_done, 1)
                c = chunk_at(n, MIX)
                if c >= 0:
                    pe.wait_ge(gate_step, 2 * c + 2)
                    for j in range(TPC):
                        mm = pe.matmul(mixed[:, P * j:P * j + P], gated[:, c % 2, P * j:P * j + P], s.decay_w_out[:, :],
                                       start=True, stop=True)
                    mm.then_inc(mixed_done, 1)

        @block.scalar
        def _(act):
            act.wait_ge(zeroed, 2)
            for n in range(END):
                if n < N:
                    act.wait_ge(scored, n + 1)
                    if n >= 8:
                        act.wait_ge(y_done, (n - 4) // G)
                    act.activation(score[:, n % 4, :, :], most[:, n % RING, :, :], ACT.Copy)\
                       .then_inc(copied, 1)
                c = chunk_at(n, COPY)
                if c >= 0:
                    act.wait_ge(y_done, TPC * (c + 1))
                    act.activation(y[:, c % 2, :], y_bank[:, c % 2, :], ACT.Copy).then_inc(y_copied, 1)
                c = chunk_at(n, SQUARE)
                if c >= 0:
                    act.wait_ge(centered, c + 1)
                    act.activation(square[:, :], y[:, c % 2, :], ACT.Square).then_inc(squared, 1)
                c = chunk_at(n, STD)
                if c >= 0:
                    act.wait_ge(var_done, c + 1)
                    act.activation(std[:, :], moment[:, :], ACT.Sqrt, bias=eps[:, :]).then_inc(std_done, 1)

        @block.vector
        def _(dve):
            rest_holds = s.rest_holds[:, :].unsqueeze(1).to_broadcast([P, HQ, HALF])
            for n in range(END):
                t, g = n // G, n % G
                if n == 0:
                    for m in range(AHEAD):
                        spread(dve, m, 0).then_inc(fwd_spread, 1)
                if n + AHEAD < N:
                    if n + AHEAD >= 2 * G:
                        dve.wait_ge(scored, n + AHEAD - 2 * G + 1)
                    spread(dve, n + AHEAD, 0).then_inc(fwd_spread, 1)
                if n < N:
                    dve.wait_ge(copied, n + 1)
                    own = rest[:, n % 2, 0:HQ * HALF].rearrange("p (h i) -> p h i", h=HQ)
                    for half in (slice(0, HALF), slice(HALF, P)):
                        merge = dve.copy_predicated(score[half, n % 4, :, half], rest_holds[half], own[half])
                    merge.then_inc(merged, 1)
                c = chunk_at(n, CENTER)
                if c >= 0:
                    dve.wait_ge(mean_done, c + 1)
                    yc = y[:, c % 2, :]
                    dve.tensor_tensor(yc, yc, moment[:, :], ALU.subtract).then_inc(centered, 1)
                for j in range(TPC):
                    c = chunk_at(n, INVERT + j)
                    if c >= 0:
                        dve.wait_ge(std_done, c + 1)
                        dve.reciprocal(rstd[:, P * j:P * j + P], std[:, P * j:P * j + P]).then_inc(inverted, 1)
                c = chunk_at(n, GATE)
                if c >= 0:
                    yc, at = y[:, c % 2, :], slice(512 * c, 512 * c + 512)
                    dve.wait_ge(inverted, TPC * (c + 1))
                    dve.scalar_tensor_tensor(out=yc, in0=yc, scalar=s.maa[:, 7:8], in1=rstd[:, :],
                                             op0=ALU.mult, op1=ALU.mult).then_inc(gate_step, 1)
                    dve.wait_ge(gate_step, 2 * c + 1)
                    if c >= 2:
                        dve.wait_ge(mixed_done, c - 1)
                    dve.scalar_tensor_tensor(out=gated[:, c % 2, :], in0=yc, scalar=s.maa[:, 8:9], in1=a.g[:, at],
                                             op0=ALU.add, op1=ALU.mult).then_inc(gate_step, 1)
                c = chunk_at(n, ADD)
                if c >= 0:
                    dve.wait_ge(mixed_done, c + 1)
                    xk = free(s.x[:, TPC * c:TPC * c + TPC, :])
                    dve.tensor_tensor(xk, mixed[:, :], xk, ALU.add).then_inc(added, 1)


def decay_attention_phase(nc, s, d, tag):
    with ExitStack() as ctx:
        def sb(name, shape):
            return ctx.enter_context(nc.sbuf_tensor(f"{tag}_{name}", shape, F32))

        a = Store()
        a.v, a.g = sb("v", [P, NT, P]), sb("g", [P, B * T])
        a.qf, a.kf, a.qb, a.kb = (sb(n, [P, B * T]) for n in ("qf", "kf", "qb", "kb"))
        with nc.sbuf_tensor(f"{tag}_r", [P, B * T], F32) as a.r, nc.sbuf_tensor(f"{tag}_k", [P, B * T], F32) as a.k, \
                nc.sbuf_tensor(f"{tag}_rate", [P, B * T], F32) as a.rate:
            mix_phase(nc, s, a, f"{tag}_mix")
            decay_phase(nc, s, a, f"{tag}_decay")
        a.state = sb("state", [P, 2, NT, P])
        state_phase(nc, s, a, f"{tag}_state")
        chunk_phase(nc, s, a, f"{tag}_chunk")


def softmax_attention_phase(nc, s, d, tag):
    PAIRS, DK = 8, 64
    TB = T // P
    ORDER = [7, 0, 6, 1, 5, 2, 4, 3]
    STEPS = [(b, i, h) for b in range(B) for i in ORDER for h in range(2)]
    N = len(STEPS)
    NP = 8
    NT_BUF = 4
    BANKS, FREED, bank = [], [], 0
    for n, (b, i, h) in enumerate(STEPS * 2):
        width = i // 4 + 1
        assert bank % 4 + width <= 4
        BANKS.append(bank % 4)
        used = range(bank % 4, bank % 4 + width)
        FREED.append(max([m - N for m in range(n) if any(BANKS[m] <= u <= BANKS[m] + STEPS[m % N][1] // 4 for u in used)],
                         default=None))
        bank += width
    assert BANKS[:N] == BANKS[N:]
    BANKS, FREED = BANKS[:N], FREED[N:]
    QUADS, quad = [], 0
    for b, i, h in STEPS:
        QUADS.append([(quad + z, 4 * z, min(4 * z + 4, i + 1)) for z in range(i // 4 + 1)])
        quad += i // 4 + 1
    NQ = quad
    UNITS = [(kk, kind) for kk in range(2) for kind in range(2)]
    NU = len(UNITS)
    NV = 2
    assert NQ % 2 == 0
    NORM_LAG, TURN_LAG, PV_LAG = 2, 5, 6
    COPY_LAG, HEAD_LAG = TURN_LAG + 1, PV_LAG + 1
    BANK_LAG = 1
    ROUND_LAG, LO_LAG = 3, 4
    JOBS = {}
    for half, rope_at, v_at in ((1, (1, 3, 5, 8), (11, 13)), (2, (17, 19, 21, 24), (27, 29))):
        for u, n in enumerate(rope_at):
            JOBS.setdefault(n, []).append(("rope", half, u))
            JOBS.setdefault(n + ROUND_LAG, []).append(("hi", half, u))
            JOBS.setdefault(n + LO_LAG, []).append(("lo", half, u))
        for g, n in enumerate(v_at):
            JOBS.setdefault(n, []).append(("v", half, g))
    NJ = NU + NV
    for b, mix_at in ((1, (7, 9)), (0, (23, 25))):
        for g, n in enumerate(mix_at):
            JOBS.setdefault(n, []).append(("mix", b, g))
    BANK_JOBS = [job for n in sorted(JOBS) for job in JOBS[n] if job[0] in ("rope", "v", "mix")]
    LAST_MIX = max(n for n in JOBS if ("mix", 1, 1) in JOBS[n])
    with ExitStack() as ctx:
        def sem(name):
            return s.semaphores.enter_context(nc.semaphore(f"{tag}_{name}"))

        def sb(name, shape, dt=F32):
            return ctx.enter_context(nc.sbuf_tensor(f"{tag}_{name}", shape, dt))

        def ps(name, shape):
            return ctx.enter_context(nc.psum_tensor(f"{tag}_{name}", shape, F32))

        w_in, w_out = sb("w_in", [P, 3, P]), sb("w_out", [P, D])
        q = sb("q", [P, 2, B, T], F32R)
        k = sb("k", [P, 2, 2, B, T], F32R)
        roped = sb("roped", [P, 2, 512])
        v = sb("v", [P, NT, P])
        by_cos, by_sin = sb("by_cos", [P, 2, 512]), sb("by_sin", [P, 2, 512])
        prob = sb("prob", [P, NP, T])
        probT = sb("probT", [P, NT_BUF, T])
        headT = sb("headT", [P, NT, P])
        neg_max, total, inverse = sb("neg_max", [P, N]), sb("total", [P, N]), sb("inverse", [P, N])
        score = ps("score", [P, 4 * 512])
        turned = ps("turned", [P, 2, 512])
        projected = ps("projected", [P, 512])
        out = ps("out", [P, 4, P])
        w_in_loaded, w_out_loaded = sem("w_in_loaded"), sem("w_out_loaded")
        projection_copied = sem("projection_copied")
        proj_done, v_done, rope_step, rope_done = sem("proj_done"), sem("v_done"), sem("rope_step"), sem("rope_done")
        hi_done, lo_done, k_moved = sem("hi_done"), (sem("a_lo_done"), sem("b_lo_done")), sem("k_moved")
        score_done, max_done, exp_done, inverse_done, prob_done = (sem("score_done"), sem("max_done"), sem("exp_done"),
                                                                   sem("inverse_done"), sem("prob_done"))
        turned_done, copied, pv_done = sem("turned_done"), [sem("even_copied"), sem("odd_copied")], sem("pv_done")
        head_copied, mixed_done = sem("head_copied"), sem("mixed_done")
        EXP0, TURNED0, COPIED0, PV0, HEAD0 = 4, NQ, 1, NT_BUF, 1
        block = ctx.enter_context(nc.Block())

        OWN = (slice(0, DK), slice(DK, P))

        def hi_of(unit, head):
            half, u = unit
            kk, kind = UNITS[u]
            at = slice(512 * kk, 512 * kk + 512)
            return q[OWN[head], head, half % 2, at] if kind == 0 else k[OWN[head], head, 0, half % 2, at]

        def lo_of(unit, head):
            half, u = unit
            kk, kind = UNITS[u]
            at = slice(512 * kk, 512 * kk + 512)
            return q[OWN[1 - head], head, half % 2, at] if kind == 0 else k[OWN[head], head, 1, half % 2, at]

        def take_lo(eng, unit, head):
            return eng.tensor_tensor(lo_of(unit, head), roped[OWN[head], unit[1] % 2, :], hi_of(unit, head).bitcast(F32),
                                     ALU.subtract)

        def jobs_before(p, job):
            kind, half, number = job
            if kind != "mix" and half == 0:
                return number if kind == "rope" else NU + number
            before = BANK_JOBS[:BANK_JOBS.index(job)]
            if isinstance(p, int) and p == 0:
                return NJ + len([j for j in before if j[:2] != ("mix", 1)])
            return p * len(BANK_JOBS) + (NJ - 2 + len(before))

        def last_quad(step):
            return QUADS[step][-1][0] + 1

        def pairs(eng, steps):
            steps(0, None)
            with eng.Fori(1, PAIRS) as p:
                steps(p, p - 1)
            steps(None, PAIRS - 1)

        def count(p):
            return N if p is not None else LAST_MIX + BANK_LAG + 1

        def lagging(p, before, n, lag):
            if n >= lag:
                return [(p, n - lag)] if p is not None else []
            return [(before, n - lag + N)] if before is not None else []

        def jobs(p, before, n, kinds):
            out = []
            for job in JOBS.get(n, []):
                pair = before if job[:2] == ("mix", 1) else p
                if job[0] in kinds and pair is not None:
                    out.append((pair, job))
            return out

        def mix_before(pair, p, job):
            return jobs_before(pair, job) if pair is not None else PAIRS * len(BANK_JOBS) + (NJ - 2 + job[2])

        @block.sync
        def _(sp):
            def load_in(p):
                sp.dma_start(w_in[:, :, :].rearrange("p a b -> p (a b)"),
                             d["attn_in"][bass.ds(p, 1), :, :].rearrange("a p w -> p (a w)")).then_inc(w_in_loaded, 16)

            def load_out(p):
                sp.dma_start(w_out[:, :], d["attn_out"][bass.ds(p, 1), :, :].rearrange("a p w -> p (a w)"))\
                  .then_inc(w_out_loaded, 16)

            def move_k(p, half):
                for u in range(NU):
                    kk, kind = UNITS[u]
                    if kind == 1:
                        at = slice(512 * kk, 512 * kk + 512)
                        for head in range(2):
                            sp.wait_ge(lo_done[head], (p * 2 + half) * NU + (u + 1))
                            sp.dma_start(k[OWN[1 - head], head, :, half % 2, at].bitcast(F32),
                                         k[OWN[head], head, :, half % 2, at].bitcast(F32)).then_inc(k_moved, 16)

            load_in(0)
            load_out(0)
            move_k(0, 0)
            with sp.Fori(0, PAIRS - 1) as p:
                move_k(p, 1)
                sp.wait_ge(v_done, p * (2 * NV) + 2 * NV)
                sp.wait_ge(w_in_loaded, p * 16 + 16)
                load_in(p + 1)
                move_k(p, 2)
                sp.wait_ge(mixed_done, p * 4 + 4)
                sp.wait_ge(w_out_loaded, p * 16 + 16)
                load_out(p + 1)
            move_k(PAIRS - 1, 1)
            sp.wait_ge(v_done, PAIRS * 2 * NV)
            sp.wait_ge(w_in_loaded, PAIRS * 16)
            load_in(PAIRS)
            move_k(PAIRS - 1, 2)
            sp.wait_ge(k_moved, 16 * 4 * (2 * PAIRS + 1))

        @block.gpsimd
        def _(pool):
            for semaphore, free_at in ((exp_done, EXP0), (turned_done, TURNED0), (copied[0], COPIED0), (copied[1], COPIED0), (pv_done, PV0), (head_copied, HEAD0)):
                pool.sem_inc(semaphore, free_at)
            pool.wait_ge(s.tables_loaded, 16)

            def rope(p, job):
                _, half, u = job
                kk, kind = UNITS[u]
                b, at = half % 2, slice(512 * kk, 512 * kk + 512)
                H = p * 2 + half
                pool.wait_ge(projection_copied, jobs_before(p, job) + 1)
                pool.tensor_tensor(by_sin[:, u % 2, :], by_sin[:, u % 2, :], s.rope[:, 2 * kind + 1, at], ALU.mult)\
                    .then_inc(rope_step, 1)
                pool.wait_ge(rope_step, H * NU + (u + 1))
                if half > 0 or u >= 2:
                    for head in range(2):
                        pool.wait_ge(lo_done[head], H * NU + (u - 1))
                pool.tensor_tensor(roped[:, u % 2, :], by_cos[:, u % 2, :], by_sin[:, u % 2, :], ALU.add).then_inc(rope_done, 1)
                pool.wait_ge(hi_done, 2 * (H * NU) + 2 * (u + 1))
                take_lo(pool, (half, u), 1).then_inc(lo_done[1], 1)
                pool.wait_ge(lo_done[1], H * NU + (u + 1))

            for u in range(NU):
                rope(0, ("rope", 0, u))
            def steps(p, before):
                for n in range(count(p)):
                    for pair, job in jobs(p, before, n, ("rope",)):
                        rope(pair, job)

            pairs(pool, steps)

        @block.tensor
        def _(pe):
            def project(p, job):
                kind_of_job, half, number = job
                b, H = half % 2, p * 2 + half
                pe.wait_ge(w_in_loaded, (p + half // 2) * 16 + 16)
                if job != ("rope", 0, 0):
                    pe.wait_ge(projection_copied, jobs_before(p, job))
                if kind_of_job == "rope":
                    kk, kind = UNITS[number]
                    pe.matmul(projected[:, :], w_in[:, kind, :], token_chunk(s.xT, 2 * b + kk), start=True, stop=True)\
                      .then_inc(proj_done, 1)
                else:
                    for j in range(TPC):
                        mm = pe.matmul(projected[:, P * j:P * j + P], token_tile(s.xT, TB * b + TPC * number + j),
                                       w_in[:, 2, :], start=True, stop=True)
                    mm.then_inc(v_done, 1)

            def scores(p, n):
                b, i, h = STEPS[n]
                if n % (N // 2) == 0:
                    for head in range(2):
                        pe.wait_ge(lo_done[head], (p * 2 + b) * NU + NU)
                    pe.wait_ge(k_moved, (p * 2 + b) * 64 + 64)
                pe.wait_ge(exp_done, p * N + (FREED[n] + 1 + EXP0))
                cols, base = P * (i + 1), 512 * BANKS[n]
                for at in range(0, cols, 512):
                    upto = min(at + 512, cols)
                    end = max(upto, at + 2 * P)
                    for part in range(2):
                        pe.matmul(score[:, base + at:base + end], q[:, h, b, P * i:P * i + P], k[:, h, part, b, at:end],
                                  start=(part == 0), stop=(part == 1 and upto < cols), skip_group_check=True)
                pe.matmul(score[:, base + P * i:base + P * i + P], s.ident_bf[:, :], s.causal[:, :], start=False, stop=True,
                          skip_group_check=True).then_inc(score_done, 1)

            def turn(p, n):
                pe.wait_ge(prob_done, p * N + (n + 1))
                for z, lo, hi in QUADS[n]:
                    pe.wait_ge(copied[z % 2], p * (NQ // 2) + (z // 2 + COPIED0))
                    for kb in range(lo, hi):
                        mm = pe.transpose(turned[:, z % 2, P * (kb - lo):P * (kb - lo) + P],
                                          prob[:, n % NP, P * kb:P * kb + P], s.ident[:, :])
                    mm.then_inc(turned_done, 1)

            def times_v(p, n):
                b, i, h = STEPS[n]
                m = n // 2
                if n % (N // 2) == 0:
                    last_v = ("v", 1 if b else 2, NV - 1)
                    if b:
                        pe.wait_ge(projection_copied, jobs_before(p, last_v) + 1)
                    elif isinstance(p, int) and p == 0:
                        pe.wait_ge(projection_copied, NJ)
                    else:
                        pe.wait_ge(projection_copied, (p - 1) * len(BANK_JOBS) + (NJ - 1 + BANK_JOBS.index(last_v)))
                if h == 0:
                    pe.wait_ge(head_copied, p * (N // 2) + (m + HEAD0))
                for z, lo, hi in QUADS[n]:
                    pe.wait_ge(copied[z % 2], p * (NQ // 2) + (z // 2 + 1 + COPIED0))
                    for kb in range(lo, hi):
                        mm = pe.matmul(out[DK * h:DK * h + DK, m % 4, :], v[:, TB * b + kb, DK * h:DK * h + DK],
                                       probT[:, n % NT_BUF, P * kb:P * kb + P], start=(kb == 0), stop=(kb == i))
                mm.then_inc(pv_done, 1)

            def mix(issuer, p, job):
                _, b, g = job
                pe.wait_ge(w_out_loaded, p * 16 + 16)
                pe.wait_ge(head_copied, p * (N // 2) + (N // 4 * (b + 1) + HEAD0))
                pe.wait_ge(projection_copied, mix_before(issuer, p, job))
                for j in range(TPC):
                    mm = pe.matmul(projected[:, P * j:P * j + P], headT[:, TB * b + TPC * g + j, :], w_out[:, :],
                                   start=True, stop=True)
                mm.then_inc(mixed_done, 1)

            for u in range(NU):
                project(0, ("rope", 0, u))
            for g in range(NV):
                project(0, ("v", 0, g))

            def steps(p, before):
                for n in range(count(p)):
                    if p is not None:
                        scores(p, n)
                    for pair, job in jobs(p, before, n, ("rope", "v", "mix")):
                        if job[0] == "mix":
                            mix(p, pair, job)
                        else:
                            project(pair, job)
                    for pair, m in lagging(p, before, n, TURN_LAG):
                        turn(pair, m)
                    for pair, m in lagging(p, before, n, PV_LAG):
                        times_v(pair, m)

            pairs(pe, steps)

        def copy_quad(eng, copy, p, n, which):
            for z, lo, hi in QUADS[n]:
                if z % 2 == which:
                    eng.wait_ge(turned_done, p * NQ + (z + 1 + TURNED0))
                    eng.wait_ge(pv_done, p * N + (n - NT_BUF + 1 + PV0))
                    copy(probT[:, n % NT_BUF, P * lo:P * hi], turned[:, which, 0:P * (hi - lo)]).then_inc(copied[which], 1)

        @block.scalar
        def _(act):
            def copy(out, in_):
                return act.activation(out, in_, ACT.Copy)

            def copy_v(p, job):
                _, half, g = job
                at = TB * (half % 2) + TPC * g
                act.wait_ge(v_done, (p * 2 + half) * NV + (g + 1))
                copy(free(v[:, at:at + TPC, :]), projected[:, :]).then_inc(projection_copied, 1)

            def take_hi(p, job):
                _, half, u = job
                act.wait_ge(rope_done, (p * 2 + half) * NU + (u + 1))
                for head in range(2):
                    copy(hi_of((half, u), head), roped[OWN[head], u % 2, :]).then_inc(hi_done, 1)

            for u in range(NU):
                take_hi(0, ("hi", 0, u))
            for g in range(NV):
                copy_v(0, ("v", 0, g))

            def exp(p, n):
                i = STEPS[n][1]
                act.wait_ge(max_done, p * N + (n + 1))
                before = last_quad(n - NP) + TURNED0 if n >= NP else last_quad(n - NP + N) + TURNED0 - NQ
                act.wait_ge(turned_done, p * NQ + before)
                act.activation(prob[:, n % NP, 0:P * (i + 1)], score[:, 512 * BANKS[n]:512 * BANKS[n] + P * (i + 1)], ACT.Exp,
                               bias=neg_max[:, n:n + 1], accum_out=total[:, n:n + 1]).then_inc(exp_done, 1)

            def steps(p, before):
                for n in range(count(p)):
                    for pair, m in lagging(p, before, n, COPY_LAG):
                        copy_quad(act, copy, pair, m, 0)
                    for pair, m in lagging(p, before, n, HEAD_LAG):
                        if m % 2 == 1:
                            b, i, h = STEPS[m]
                            act.wait_ge(pv_done, pair * N + (m + 1 + PV0))
                            copy(headT[:, TB * b + i, :], out[:, m // 2 % 4, :]).then_inc(head_copied, 1)
                    for pair, job in jobs(p, before, n - BANK_LAG, ("v",)):
                        copy_v(pair, job)
                    if p is not None:
                        exp(p, n)
                    for pair, job in jobs(p, before, n, ("hi",)):
                        take_hi(pair, job)

            pairs(act, steps)

        @block.vector
        def _(dve):
            def add_mixed(p, job):
                _, b, g = job
                c = 2 * b + g
                dve.wait_ge(mixed_done, p * 4 + (c + 1))
                xk = free(s.x[:, TPC * c:TPC * c + TPC, :])
                dve.tensor_tensor(xk, projected[:, :], xk, ALU.add).then_inc(projection_copied, 1)

            HALVES_SWAPPED = list(range(16, 32)) + list(range(16))

            def rope(p, job):
                _, half, u = job
                kk, kind = UNITS[u]
                unit = (p * 2 + half) * NU + u
                dve.wait_ge(proj_done, unit + 1)
                if half > 0 or u >= 2:
                    dve.wait_ge(rope_done, unit - 1)
                dve.tensor_tensor(by_cos[:, u % 2, :], projected[:, :], s.rope[:, 2 * kind, 512 * kk:512 * kk + 512], ALU.mult)
                dve.stream_shuffle(by_sin[:, u % 2, :], projected[:, :], HALVES_SWAPPED).then_inc(projection_copied, 1)

            def lo(p, job):
                _, half, u = job
                dve.wait_ge(hi_done, (p * 2 + half) * (2 * NU) + 2 * (u + 1))
                take_lo(dve, (half, u), 0).then_inc(lo_done[0], 1)

            dve.wait_ge(s.tables_loaded, 16)
            for u in range(NU):
                rope(0, ("rope", 0, u))
                if u >= 1:
                    lo(0, ("lo", 0, u - 1))
            lo(0, ("lo", 0, NU - 1))

            def invert(p, m):
                dve.wait_ge(exp_done, p * N + (m + 1 + EXP0))
                dve.reciprocal(inverse[:, m:m + 1], total[:, m:m + 1]).then_inc(inverse_done, 1)

            def scale(p, m):
                dve.wait_ge(inverse_done, p * N + (m + 1))
                row = prob[:, m % NP, 0:P * (STEPS[m][1] + 1)]
                dve.tensor_scalar(row, row, inverse[:, m:m + 1], None, ALU.mult).then_inc(prob_done, 1)

            def row_max(p, n):
                i = STEPS[n][1]
                dve.wait_ge(score_done, p * N + (n + 1))
                dve.tensor_reduce(neg_max[:, n:n + 1], score[:, 512 * BANKS[n]:512 * BANKS[n] + P * (i + 1)], AX_X, ALU.max,
                                  negate=True).then_inc(max_done, 1)

            def steps(p, before):
                for n in range(count(p)):
                    for pair, m in lagging(p, before, n, NORM_LAG):
                        invert(pair, m)
                    for pair, m in lagging(p, before, n, COPY_LAG):
                        copy_quad(dve, dve.tensor_copy, pair, m, 1)
                    for pair, m in lagging(p, before, n, NORM_LAG):
                        scale(pair, m)
                    for pair, job in jobs(p, before, n - BANK_LAG, ("rope", "mix")):
                        (rope if job[0] == "rope" else add_mixed)(pair, job)
                    if p is not None:
                        row_max(p, n)
                    for pair, job in jobs(p, before, n, ("lo",)):
                        lo(pair, job)

            pairs(dve, steps)


def expert_ffn_phase(nc, s, d, tag):
    E, R, F, TOP = 17, 15, 256, 3
    S = E - R
    W1, W2 = 2, 2 + F
    ROW = 2 + 2 * F
    with ExitStack() as ctx:
        def sem(name):
            return s.semaphores.enter_context(nc.semaphore(f"{tag}_{name}"))

        def sb(name, shape, dt=F32):
            return ctx.enter_context(nc.sbuf_tensor(f"{tag}_{name}", shape, dt))

        def ps(name, shape):
            return ctx.enter_context(nc.psum_tensor(f"{tag}_{name}", shape, F32))

        weights = sb("weights", [P, 2, ROW])
        w_hi, w_lo = sb("w_hi", [P, 2, F], F32R), sb("w_lo", [P, 2, F], F32R)
        zeros = sb("zeros", [P, F])
        n_hi, n_lo = sb("n_hi", [P, NC, 512], F32R), sb("n_lo", [P, NC, 512], F32R)
        hidden = sb("hidden", [P, 2, 2, 512])
        acc = sb("acc", [P, NT, D])
        score, prob = sb("score", [P, NT, R]), sb("prob", [P, NT, R])
        beats, rank = sb("beats", [P, NT, R, R]), sb("rank", [P, NT, R])
        top, total, inverse = sb("top", [P, NT]), sb("total", [P, NT]), sb("inverse", [P, NT])
        gates = sb("gates", [P, E, NT])
        gatesT = sb("gatesT", [P, NT * P])
        up = ps("up", [P, 2, 2, 512])
        down = ps("down", [P, 2, 512])
        side = ps("side", [P, 2, 512])
        w_loaded = [sem("w0_loaded"), sem("w1_loaded")]
        w_rounded, w_split, n_rounded, n_split = sem("w_rounded"), sem("w_split"), sem("n_rounded"), sem("n_split")
        logits_done, gate_step, exp_done, gates_done = sem("logits_done"), sem("gate_step"), sem("exp_done"), sem("gates_done")
        zeroed, turned_done, turned_copied = sem("zeroed"), sem("turned_done"), sem("turned_copied")
        bias_done, bias_added = sem("bias_done"), sem("bias_added")
        up_done, gelu_done, down_done, acc_done = sem("up_done"), sem("gelu_done"), sem("down_done"), sem("acc_done")
        block = ctx.enter_context(nc.Block())
        logits = side[:, 0, 0:NT * R].rearrange("p (t e) -> p t e", e=R)

        @block.sync
        def _(sp):
            def load(e, parity):
                sp.dma_start(weights[:, parity, :], d["experts"][bass.ds(e, 1), :, :].rearrange("a p w -> p (a w)"))\
                  .then_inc(w_loaded[parity], 16)

            load(0, 0)
            load(1, 1)
            with sp.Fori(0, (E - 3) // 2) as i:
                sp.wait_ge(down_done, i * 8 + 4)
                sp.wait_ge(w_loaded[0], i * 16 + 16)
                load(i * 2 + 2, 0)
                sp.wait_ge(down_done, i * 8 + 8)
                sp.wait_ge(w_loaded[1], i * 16 + 16)
                load(i * 2 + 3, 1)
            sp.wait_ge(down_done, 4 * (E - 2))
            sp.wait_ge(w_loaded[0], 16 * (E - 1) // 2)
            load(E - 1, 0)

        @block.gpsimd
        def _(pool):
            def split(parity, e):
                w1 = weights[:, parity, W1:W1 + F]
                pool.tensor_tensor(w_hi[:, parity, :], w1, zeros[:, :], ALU.add).then_inc(w_rounded, 1)
                pool.wait_ge(w_rounded, e + 1)
                pool.tensor_tensor(w_lo[:, parity, :], w1, w_hi[:, parity, :].bitcast(F32), ALU.subtract).then_inc(w_split, 1)

            pool.memset(zeros[:, :], 0.0).then_inc(zeroed, 1)
            pool.wait_ge(zeroed, 1)
            pool.wait_ge(w_loaded[0], 16)
            split(0, 0)
            pool.memset(gates[:, 0:S, :], 1.0).then_inc(zeroed, 1)
            pool.memset(gatesT[:, :], 0.0).then_inc(zeroed, 1)
            pool.memset(beats[:, :, :, :], 0.0).then_inc(zeroed, 1)
            pool.wait_ge(w_loaded[1], 16)
            split(1, 1)
            with pool.Fori(0, (E - 3) // 2) as i:
                for parity in range(2):
                    pool.wait_ge(up_done, i * 16 + 8 * (parity + 1))
                    pool.wait_ge(w_loaded[parity], i * 16 + 32)
                    split(parity, i * 2 + (2 + parity))
            pool.wait_ge(up_done, 8 * (E - 2))
            pool.wait_ge(w_loaded[0], 16 * (E + 1) // 2)
            split(0, E - 1)

        @block.tensor
        def _(pe):
            for t in range(NT):
                mm = pe.matmul(logits[:, t, :], token_tile(s.xT, t), s.gate_w[:, :], start=True, stop=True)
            mm.then_inc(logits_done, 1)

            def up_chunk(n, k, parity):
                for m in range(2):
                    cols = slice(P * m, P * m + P)
                    pe.matmul(up[:, k % 2, m, :], w_hi[:, parity, cols], n_hi[:, k, :], start=True, stop=False)
                    pe.matmul(up[:, k % 2, m, :], w_hi[:, parity, cols], n_lo[:, k, :], start=False, stop=False)
                    pe.matmul(up[:, k % 2, m, :], w_lo[:, parity, cols], n_hi[:, k, :], start=False, stop=True)\
                      .then_inc(up_done, 1)

            def down_chunk(k, parity):
                for j in range(TPC):
                    for m in range(2):
                        mm = pe.matmul(down[:, k % 2, P * j:P * j + P], hidden[:, k % 2, m, P * j:P * j + P],
                                       weights[:, parity, W2 + P * m:W2 + P * m + P], start=(m == 0), stop=(m == 1))
                mm.then_inc(down_done, 1)

            pe.wait_ge(w_split, 1)
            for k in range(NC):
                pe.wait_ge(n_split, k + 1)
                if k >= 2:
                    pe.wait_ge(gelu_done, 2 * (k - 1))
                up_chunk(k, k, 0)
                if k >= 1:
                    pe.wait_ge(gelu_done, 2 * k)
                    if k >= 3:
                        pe.wait_ge(acc_done, k - 2)
                    down_chunk(k - 1, 0)
            pe.wait_ge(gates_done, 1)
            pe.wait_ge(zeroed, 4)
            for g in range(NC):
                if g >= 2:
                    pe.wait_ge(turned_copied, g - 1)
                for j in range(TPC):
                    turn = pe.transpose(side[0:E, g % 2, P * j:P * j + P], gates[:, :, TPC * g + j], s.ident[:, :])
                turn.then_inc(turned_done, 1)
            for g in range(NC):
                if g < 2:
                    pe.wait_ge(turned_copied, NC - 1 + g)
                else:
                    pe.wait_ge(bias_added, g - 1)
                for j in range(TPC):
                    at = 512 * g + P * j
                    mm = pe.matmul(side[:, g % 2, P * j:P * j + P], gatesT[:, at:at + P], s.expert_b2[:, :],
                                   start=True, stop=True)
                mm.then_inc(bias_done, 1)
            with pe.Fori(0, (E - 1) // 2) as i:
                for c in range(2 * NC):
                    k = c % NC
                    parity = 1 - c // NC
                    n = i * 8 + (NC + c)
                    if c % NC == 0:
                        pe.wait_ge(w_split, i * 2 + (2 + c // NC))
                    pe.wait_ge(gelu_done, (n - 1) * 2)
                    up_chunk(n, k, parity)
                    pe.wait_ge(gelu_done, n * 2)
                    pe.wait_ge(acc_done, n - 2)
                    down_chunk((k - 1) % NC, parity if k else 1 - parity)
            pe.wait_ge(gelu_done, 2 * E * NC)
            pe.wait_ge(acc_done, E * NC - 2)
            down_chunk(NC - 1, 0)

        @block.scalar
        def _(act):
            def gelu_chunk(n, k, parity):
                for m in range(2):
                    act.wait_ge(up_done, n * 2 + (m + 1))
                    act.activation(hidden[:, k % 2, m, :], up[:, k % 2, m, :], ACT.Gelu,
                                   bias=weights[:, parity, m:m + 1]).then_inc(gelu_done, 1)

            for k in range(NC):
                act.activation(n_hi[:, k, :], token_chunk(s.xT, k), ACT.Copy).then_inc(n_rounded, 1)
            act.wait_ge(gate_step, 3)
            act.activation(prob[:, :, :], score[:, :, :], ACT.Exp).then_inc(exp_done, 1)
            for k in range(NC):
                if k >= 2:
                    act.wait_ge(down_done, k - 1)
                gelu_chunk(k, k, 0)
            for g in range(NC):
                act.wait_ge(turned_done, g + 1)
                act.activation(gatesT[0:E, 512 * g:512 * g + 512], side[0:E, g % 2, :], ACT.Copy).then_inc(turned_copied, 1)
            with act.Fori(0, (E - 1) // 2) as i:
                for c in range(2 * NC):
                    n = i * 8 + (NC + c)
                    act.wait_ge(down_done, n - 1)
                    gelu_chunk(n, c % NC, 1 - c // NC)

        @block.vector
        def _(dve):
            def wide(ap):
                return ap.unsqueeze(2).to_broadcast([P, NT, R])

            def add_bias(g):
                dve.wait_ge(bias_done, g + 1)
                dve.wait_ge(acc_done, g + 1)
                a = free(acc[:, TPC * g:TPC * g + TPC, :])
                dve.tensor_tensor(a, side[:, g % 2, :], a, ALU.add).then_inc(bias_added, 1)

            for k in range(NC):
                dve.wait_ge(n_rounded, k + 1)
                dve.tensor_tensor(n_lo[:, k, :], token_chunk(s.xT, k), n_hi[:, k, :].bitcast(F32), ALU.subtract)\
                   .then_inc(n_split, 1)
            dve.wait_ge(logits_done, 1)
            dve.tensor_tensor(score[:, :, :], logits, s.gate_b[:, :].unsqueeze(1).to_broadcast([P, NT, R]), ALU.add)\
               .then_inc(gate_step, 1)
            dve.wait_ge(gate_step, 1)
            dve.tensor_reduce(top[:, :], score[:, :, :], AX_X, ALU.max).then_inc(gate_step, 1)
            dve.wait_ge(gate_step, 2)
            dve.tensor_tensor(score[:, :, :], score[:, :, :], wide(top[:, :]), ALU.subtract).then_inc(gate_step, 1)
            dve.wait_ge(exp_done, 1)
            dve.tensor_reduce(total[:, :], prob[:, :, :], AX_X, ALU.add).then_inc(gate_step, 1)
            dve.wait_ge(gate_step, 4)
            dve.reciprocal(inverse[:, :], total[:, :]).then_inc(gate_step, 1)
            dve.wait_ge(gate_step, 5)
            dve.tensor_tensor(prob[:, :, :], prob[:, :, :], wide(inverse[:, :]), ALU.mult).then_inc(gate_step, 1)
            dve.wait_ge(gate_step, 6)
            dve.wait_ge(zeroed, 4)
            for e in range(R):
                if e > 0:
                    dve.tensor_tensor(beats[:, :, e, 0:e], prob[:, :, 0:e],
                                      prob[:, :, e:e + 1].to_broadcast([P, NT, e]), ALU.is_ge).then_inc(gate_step, 1)
                if e < R - 1:
                    dve.tensor_tensor(beats[:, :, e, e + 1:R], prob[:, :, e + 1:R],
                                      prob[:, :, e:e + 1].to_broadcast([P, NT, R - 1 - e]), ALU.is_gt).then_inc(gate_step, 1)
            dve.wait_ge(gate_step, 6 + 2 * (R - 1))
            dve.tensor_reduce(rank[:, :, :], beats[:, :, :, :], AX_X, ALU.add).then_inc(gate_step, 1)
            dve.wait_ge(gate_step, 7 + 2 * (R - 1))
            dve.scalar_tensor_tensor(out=gates[:, S:E, :].rearrange("p e t -> p t e"), in0=rank[:, :, :], scalar=float(TOP),
                                     in1=prob[:, :, :], op0=ALU.is_lt, op1=ALU.mult).then_inc(gates_done, 1)
            for k in range(NC):
                dve.wait_ge(down_done, k + 1)
                dve.tensor_tensor(free(acc[:, TPC * k:TPC * k + TPC, :]), down[:, k % 2, :],
                                  free(s.normed[:, TPC * k:TPC * k + TPC, :]), ALU.add).then_inc(acc_done, 1)
                if k == NC - 2:
                    for g in range(NC - 1):
                        add_bias(g)
            add_bias(NC - 1)
            dve.wait_ge(bias_added, NC)
            with dve.Fori(0, (E - 1) // 2) as i:
                for c in range(2 * NC):
                    k = c % NC
                    n = i * 8 + (NC + c)
                    dve.wait_ge(down_done, n + 1)
                    dve.wait_ge(acc_done, n - 3)
                    for j in range(TPC):
                        t = TPC * k + j
                        add = dve.scalar_tensor_tensor(out=acc[:, t, :], in0=down[:, k % 2, P * j:P * j + P],
                                                       scalar=gates[:, bass.ds(i * 2 + (1 + c // NC), 1), t],
                                                       in1=acc[:, t, :], op0=ALU.mult, op1=ALU.add)
                    add.then_inc(acc_done, 1)
            for k in range(NC):
                dve.wait_ge(acc_done, (E - 1) * NC + k + 1)
                xk = free(s.x[:, TPC * k:TPC * k + TPC, :])
                dve.scalar_tensor_tensor(out=xk, in0=free(acc[:, TPC * k:TPC * k + TPC, :]), scalar=0.5, in1=xk,
                                         op0=ALU.mult, op1=ALU.add)

def layout_more(np, i):
    w1 = np.concatenate([i["L1_ffn_sW1"][:, :, :256], i["L1_ffn_sW1"][:, :, 256:], i["L1_ffn_rW1"]])
    b1 = np.concatenate([i["L1_ffn_sb1"].reshape(2, 256), i["L1_ffn_rb1"]])
    w2 = np.concatenate([i["L1_ffn_sW2"].reshape(2, 256, 128), i["L1_ffn_rW2"]])
    experts = np.concatenate([b1.reshape(17, 2, 128).transpose(0, 2, 1), w1,
                              w2.reshape(17, 2, 128, 128).transpose(0, 2, 1, 3).reshape(17, 128, 256)], axis=2)
    b2 = np.zeros((128, 128), np.float32)
    b2[0] = i["L1_ffn_sb2"][0]
    b2[2:17] = i["L1_ffn_rb2"]
    inv_freq = (1.0 / np.float32(6000.0) ** (np.arange(0, 32, 2, dtype=np.float32) / np.float32(32))).astype(np.float32)
    angle = np.outer(np.arange(1024, dtype=np.float32), inv_freq).astype(np.float32)
    cos, sin = np.cos(angle).T, np.sin(angle).T
    one, none = np.ones((32, 1024), np.float32), np.zeros((32, 1024), np.float32)
    c = np.concatenate([cos, cos, one] * 2)
    sn = np.concatenate([-sin, sin, none] * 2)
    rope = np.stack([c / 8, sn / 8, c, sn], axis=1).astype(np.float32)
    wq, wk, wv = i["L1_attn_W_qkv"]
    attn_in = np.zeros((9, 128, 3, 128), np.float32)
    for n, w in enumerate((wq, wk, wv)):
        attn_in[:8, :, n] = w.reshape(8, 128, 128).transpose(0, 2, 1)
    attn_out = i["L1_attn_W_o"].reshape(128, 8, 128).transpose(1, 2, 0)
    causal = np.triu(np.full((128, 128), -1e30, np.float32), 1)
    vec = lambda name: i["L0_attn_" + name].reshape(128)
    maa = np.stack([vec("time_maa_" + f) for f in "wkvrgx"] + [vec("time_decay"), vec("ln_w"), vec("ln_b")], axis=1)
    maa_w1 = np.zeros((128, 256), np.float32)
    maa_w1[:, :160] = i["L0_attn_time_maa_w1"]
    maa_w2 = np.zeros((128, 5, 128), np.float32)
    for f in range(5):
        maa_w2[32 * (f % 4):32 * (f % 4) + 32, f] = i["L0_attn_time_maa_w2"][f]
    decay_w1, decay_w2 = np.zeros((128, 128), np.float32), np.zeros((128, 128), np.float32)
    decay_w1[:, :64], decay_w2[:64] = i["L0_attn_time_decay_w1"], i["L0_attn_time_decay_w2"]
    mix_w = np.stack([decay_w1] + [i["L0_attn_W_" + f].T for f in "kvrg"], axis=1)
    head = np.arange(128) // 8
    return {
        "maa": maa,
        "maa_w1": maa_w1.reshape(128, 2, 128),
        "maa_w2": maa_w2,
        "mix_w": mix_w,
        "decay_w2": decay_w2,
        "decay_w_out": i["L0_attn_W_o"].T,
        "same_head": (head[:, None] == head[None, :]).astype(np.float32),
        "head_mean": (head[:, None] == head[None, :]).astype(np.float32) / 8,
        "head_of": (head[:, None] == np.arange(16)[None, :]).astype(np.float32),
        "rest_holds": np.concatenate([np.triu(np.ones((64, 64), np.float32)), np.tril(np.ones((64, 64), np.float32), -1)]),
        "rope": rope,
        "attn_in": attn_in.reshape(9, 128, 384),
        "attn_out": attn_out,
        "causal": causal,
        "experts": experts,
        "expert_b2": b2,
        "gate_w": i["L1_ffn_gW"],
        "gate_b": np.broadcast_to(i["L1_ffn_gb"], (128, 15)),
    }


STAGES = 6


def program(nc, d, out):
    with ExitStack() as ctx:
        def sb(name, shape, dt=F32):
            return ctx.enter_context(nc.sbuf_tensor(name, shape, dt))

        s = Store()
        s.semaphores = ctx
        s.x = sb("x", [P, NT, D])
        s.xT = sb("xT", [P, B, T + 2])
        s.normed = sb("normed", [P, NT, D])
        s.gate_w = sb("gate_w", [P, 15])
        s.gate_b = sb("gate_b", [P, 15])
        s.expert_b2 = sb("expert_b2", [P, D])
        s.rope = sb("rope", [P, 4, T])
        s.causal_f = sb("causal_f", [P, P])
        s.causal = sb("causal", [P, P], BF16)
        s.ident_bf = sb("ident_bf", [P, P], BF16)
        s.other_loaded = ctx.enter_context(nc.semaphore("other_loaded"))
        s.tables_loaded = ctx.enter_context(nc.semaphore("tables_loaded"))
        s.maa = sb("maa", [P, 9])
        s.maa_w1 = sb("maa_w1", [P, 2, P])
        s.maa_w2 = sb("maa_w2", [P, 5, P])
        s.mix_w = sb("mix_w", [P, 5, P])
        s.decay_w2 = sb("decay_w2", [P, P])
        s.decay_w_out = sb("decay_w_out", [P, P])
        s.same_head = sb("same_head", [P, P])
        s.head_mean = sb("head_mean", [P, P])
        s.head_of = sb("head_of", [P, 16])
        s.rest_holds_f = sb("rest_holds_f", [P, P // 2])
        s.rest_holds = sb("rest_holds", [P, P // 2], mybir.dt.uint8)
        s.ident = sb("ident", [P, P])
        s.w_fc = sb("w_fc", [P, 512])
        s.w_proj = sb("w_proj", [P, 4, D])
        s.ffn_ln = sb("ffn_ln", [P, 2, 4])
        load_phase(nc, s, d)
        ternary_phase(nc, s)
        steps = [lambda g: ternary_ffn_phase(nc, s, g), lambda g: decay_attention_phase(nc, s, d, g),
                 lambda g: ternary_ffn_phase(nc, s, g), lambda g: expert_ffn_phase(nc, s, d, g),
                 lambda g: softmax_attention_phase(nc, s, d, g), lambda g: expert_ffn_phase(nc, s, d, g)]
        for n, step in enumerate(steps[:STAGES]):
            if n == 1:
                masks_phase(nc, s)
            layernorm_phase(nc, s, f"norm{n}")
            step(f"layer{n}")
        store_phase(nc, s, out)


def kernel(**inputs):
    import numpy as _np
    import concourse.bacc as _bacc
    from concourse import mybir as _mybir
    from concourse.bass_utils import run_bass_kernel_spmd as _run

    i = {k: _np.asarray(v) for k, v in inputs.items()}
    lay = {
        "x": i["L0_attn_x"],
        "eye": _np.eye(128, dtype=_np.float32),
        "w_fc": i["L0_ffn_W_fc"].T,
        "w_proj": i["L0_ffn_W_proj"].T,
        "ffn_ln": _np.stack([i["L0_ffn_ln_w"].reshape(4, 128).T, i["L0_ffn_ln_b"].reshape(4, 128).T], axis=1),
    }
    lay.update(layout_more(_np, i))
    nc = _bacc.Bacc("TRN2", target_bir_lowering=False, num_devices=1)
    arrays, d = {}, {}
    for name, a in lay.items():
        a = _np.ascontiguousarray(a)
        arrays[f"in_{name}"] = a
        d[name] = nc.dram_tensor(f"in_{name}", a.shape, _mybir.dt.from_np(a.dtype), kind="ExternalInput").ap()
    out = nc.dram_tensor("out_0", (2, 1024, 128), _mybir.dt.float32, kind="ExternalOutput").ap()
    program(nc, d, out)
    r = _run(nc, [arrays], core_ids=[0])
    return r.results[0]["out_0"]
```
